# Optimizing a Trainium2 kernel written in Bass

```python
import numpy as np
import jax
import jax.numpy as jnp

def _softmax(x, axis=-1):
    return jax.nn.softmax(x, axis=axis)

def _gelu(x):
    return jax.nn.gelu(x, approximate=True)

def _silu(x):
    return jax.nn.silu(x)

def _sigmoid(x):
    return jax.nn.sigmoid(x)

def _layernorm(x, axis=-1, eps=1e-05):
    m = jnp.mean(x, axis=axis, keepdims=True)
    v = jnp.var(x, axis=axis, keepdims=True)
    return (x - m) / jnp.sqrt(v + eps)

def _scatter_add(tgt, idx, src, axis=0):
    return tgt.at[idx].add(src)

def _segment_sum(src, seg, n):
    return jax.ops.segment_sum(src, seg, n)
kernel_name = 'mk_prb_d1_jaxref_r2_836a6c'

def setup_inputs(seed: int=0):
    np.random.seed(seed)
    _w = jnp.asarray

    def _L0_attn_setup():
        import jax, jax.numpy as jnp
        import numpy as np
        N_EMBD = 512
        N_ATTN = 512
        N_HEAD = 16
        N_LAYER = 12
        LAYER_ID = 5
        CTX = 1024
        BATCH = 8
        HEAD_SIZE = N_ATTN // N_HEAD
        K_CLAMP = 60.0
        K_EPS = 1e-16

        def _time_decay_init():
            first = 1
            f1 = 3.0 + (LAYER_ID - first) / (N_LAYER - 1 - first) * (1.2 - 3.0)
            f2 = 0.65 + (LAYER_ID - first) / (N_LAYER - 1 - first) * (0.4 - 0.65)
            if LAYER_ID == first:
                f1 += 0.5
            if LAYER_ID == N_LAYER - 2:
                f2 = 0.4
            if LAYER_ID == N_LAYER - 1:
                f2 = 0.37
            h = np.arange(N_HEAD, dtype=np.float64)
            decay_speed = np.power(f2, h / (N_HEAD - 1) * 7) * f1
            return np.log(decay_speed).astype(np.float32)[:, None]
        key = jax.random.key(seed)
        ks = jax.random.split(key, 5)
        x = jax.random.normal(ks[0], (BATCH, CTX, N_EMBD), dtype=jnp.float32)
        tm = np.ones((1, 1, N_EMBD), dtype=np.float32)
        tm[0, 0, :N_EMBD // 2] = 0.0
        scale = 0.02
        return {'x': x, 'time_decay': jnp.asarray(_time_decay_init()), 'time_first': jnp.full((N_HEAD, 1), np.log(0.3), dtype=jnp.float32), 'time_mix': jnp.asarray(tm), 'Wk': jax.random.normal(ks[1], (N_ATTN, N_EMBD), dtype=jnp.float32) * scale, 'Wv': jax.random.normal(ks[2], (N_ATTN, N_EMBD), dtype=jnp.float32) * scale, 'Wr': jax.random.normal(ks[3], (N_ATTN, N_EMBD), dtype=jnp.float32) * scale, 'Wo': jax.random.normal(ks[4], (N_EMBD, N_ATTN), dtype=jnp.float32) * scale}
    _L0_attn_in = _L0_attn_setup()

    def _L0_ffn_setup():
        import jax, jax.numpy as jnp
        import numpy as np
        LN_EPS = 0.001
        EPS = 1e-05
        QB = 128.0

        def ste_round(x):
            return x + jax.lax.stop_gradient(jnp.round(x) - x)
        key = jax.random.key(seed)
        k1, k2 = jax.random.split(key)
        x = jax.random.normal(k1, (4, 4096, 512), dtype=jnp.float32)
        weight = jax.random.normal(k2, (512, 512), dtype=jnp.float32) * 0.02
        ln_gamma = jnp.ones((512,), dtype=jnp.float32)
        ln_beta = jnp.zeros((512,), dtype=jnp.float32)
        return {'x': x, 'weight': weight, 'ln_gamma': ln_gamma, 'ln_beta': ln_beta}
    _L0_ffn_in = _L0_ffn_setup()
    _d = {'L0_attn_x': _L0_attn_in['x'], 'L0_attn_time_decay': _L0_attn_in['time_decay'], 'L0_attn_time_first': _L0_attn_in['time_first'], 'L0_attn_time_mix': _L0_attn_in['time_mix'], 'L0_attn_Wk': _L0_attn_in['Wk'], 'L0_attn_Wv': _L0_attn_in['Wv'], 'L0_attn_Wr': _L0_attn_in['Wr'], 'L0_attn_Wo': _L0_attn_in['Wo'], 'L0_ffn_weight': _L0_ffn_in['weight'], 'L0_ffn_ln_gamma': _L0_ffn_in['ln_gamma'], 'L0_ffn_ln_beta': _L0_ffn_in['ln_beta']}
    _x0 = _d['L0_attn_x']
    _d['L0_attn_x'] = jax.random.normal(jax.random.fold_in(jax.random.key(seed), 1), (8, 1024, 512), dtype=_x0.dtype)
    del _x0
    return _d

def reference(L0_attn_x, L0_attn_time_decay, L0_attn_time_first, L0_attn_time_mix, L0_attn_Wk, L0_attn_Wv, L0_attn_Wr, L0_attn_Wo, L0_ffn_weight, L0_ffn_ln_gamma, L0_ffn_ln_beta):

    def _L0_attn_ref(x, time_decay, time_first, time_mix, Wk, Wv, Wr, Wo):
        import jax, jax.numpy as jnp
        import numpy as np
        N_EMBD = 512
        N_ATTN = 512
        N_HEAD = 16
        N_LAYER = 12
        LAYER_ID = 5
        CTX = 1024
        BATCH = 8
        HEAD_SIZE = N_ATTN // N_HEAD
        K_CLAMP = 60.0
        K_EPS = 1e-16

        def _time_decay_init():
            first = 1
            f1 = 3.0 + (LAYER_ID - first) / (N_LAYER - 1 - first) * (1.2 - 3.0)
            f2 = 0.65 + (LAYER_ID - first) / (N_LAYER - 1 - first) * (0.4 - 0.65)
            if LAYER_ID == first:
                f1 += 0.5
            if LAYER_ID == N_LAYER - 2:
                f2 = 0.4
            if LAYER_ID == N_LAYER - 1:
                f2 = 0.37
            h = np.arange(N_HEAD, dtype=np.float64)
            decay_speed = np.power(f2, h / (N_HEAD - 1) * 7) * f1
            return np.log(decay_speed).astype(np.float32)[:, None]
        B, T, C = x.shape
        H = time_decay.shape[0]
        D = Wk.shape[0] // H
        xs = jnp.pad(x, ((0, 0), (1, 0), (0, 0)))[:, :T]
        xm = x * time_mix + xs * (1.0 - time_mix)
        k = jnp.exp(jnp.minimum(xm @ Wk.T, K_CLAMP))
        v = xm @ Wv.T
        r = xm @ Wr.T
        kv = k * v
        lag = jnp.arange(T)[:, None] - jnp.arange(T)[None, :]
        dec = jnp.exp(time_decay[:, 0])[:, None, None]
        e = jnp.exp(-dec * jnp.maximum(lag - 1, 0).astype(jnp.float32))
        Wm = jnp.where(lag >= 1, e, 0.0)
        Wm = jnp.where(lag == 0, jnp.exp(time_first[:, 0])[:, None, None], Wm)
        kh = k.reshape(B, T, H, D)
        kvh = kv.reshape(B, T, H, D)
        wkv = jnp.einsum('htu,buhd->bthd', Wm, kvh).reshape(B, T, H * D)
        sum_k = jnp.einsum('htu,buhd->bthd', Wm, kh).reshape(B, T, H * D) + K_EPS
        rwkv = jax.nn.sigmoid(r) * wkv / sum_k
        return rwkv @ Wo.T

    def _L0_ffn_ref(x, weight, ln_gamma, ln_beta):
        import jax, jax.numpy as jnp
        import numpy as np
        LN_EPS = 0.001
        EPS = 1e-05
        QB = 128.0

        def ste_round(x):
            return x + jax.lax.stop_gradient(jnp.round(x) - x)
        mu = jnp.mean(x, axis=-1, keepdims=True)
        var = jnp.var(x, axis=-1, keepdims=True)
        xn = (x - mu) * jax.lax.rsqrt(var + LN_EPS) * ln_gamma + ln_beta
        beta = jnp.mean(jnp.abs(weight))
        w_q = jnp.clip(ste_round(weight / (beta + EPS)), -1.0, 1.0)
        gamma = jnp.max(jnp.abs(xn))
        xq = jnp.clip(xn * QB / gamma, -QB + EPS, QB - EPS)
        y = jnp.einsum('bsd,du->bsu', xq, w_q)
        return y * (gamma * beta / QB)
    x = L0_attn_x
    xn = _layernorm(x, axis=-1)
    x = x + _L0_attn_ref(xn, L0_attn_time_decay, L0_attn_time_first, L0_attn_time_mix, L0_attn_Wk, L0_attn_Wv, L0_attn_Wr, L0_attn_Wo) + _L0_ffn_ref(xn, L0_ffn_weight, L0_ffn_ln_gamma, L0_ffn_ln_beta)
    return x

_drawn_inputs = setup_inputs


def setup_inputs(seed=0):
    import zlib

    import numpy as np

    out = dict(_drawn_inputs(seed))
    spreads = {'L0_attn_time_first': (-1.2039728164672852, 0.6),
     'L0_ffn_ln_gamma': (1.0, 0.2),
     'L0_ffn_ln_beta': (0.0, 0.293)}
    factors = {'L0_attn_Wk': 4.094, 'L0_attn_Wr': 5.932}
    for name, (base, spread) in spreads.items():
        noise = np.random.default_rng([zlib.crc32(name.encode()), seed]).standard_normal(out[name].shape)
        drawn = base * np.exp(spread * noise) if base else spread * noise
        out[name] = jnp.asarray(drawn.astype(out[name].dtype))
    for name, factor in factors.items():
        out[name] = (out[name] * factor).astype(out[name].dtype)
    return out
```

```python
from contextlib import ExitStack
import math

import concourse.bass as bass
from concourse import mybir

F32 = mybir.dt.float32
F32R = mybir.dt.float32r
ALU = mybir.AluOpType
ACT = mybir.ActivationFunctionType
AX = mybir.AxisListType

P = 128
TILE = 512
LN_EPS = 1e-5
FFN_LN_EPS = 1e-3
FFN_EPS = 1e-5
QB = 128.0
K_CLAMP = 60.0
K_EPS = 1e-16

SLOT_KINDS = ["ffn_own0", "ffn_other0", "mix_own1", "ffn_own1", "ffn_other1", "mix_next0"]
SLOTS = [(kind, ch) for kind in SLOT_KINDS for ch in range(4)]
LOOP_SLOTS = 23 - 3
FFN_AFTER = {4: "own0", 8: "other0", 16: "own1", 20: "other1"}
BANK_USES = {"A": ["attn0", "attn1"],
             "B": ["own0", "other0", "attn0", "own1", "other1", "attn1"]}
ATTN0_AFTER = 12


def mixed_decay_kernel(nc, x, time_decay, time_first, time_mix, Wk, Wv, Wr, Wo, Wf, ln_gamma, ln_beta, out):
    B, T, C = x.shape
    H = time_decay.shape[0]
    CH = C // P
    Q = TILE // P
    D = C // H
    HPC = P // D
    HALF = B // 2
    assert (CH, Q, T // TILE, 2 * HALF) == (4, 4, 2, B)
    GROUPS = 2 * CH * 3
    USERS_A = 2 * CH
    USERS_B = len(SLOTS)

    x_t = x.rearrange("b (t q p) c -> b t p q c", q=Q, p=P)
    out_t = out.rearrange("b (t q p) c -> b t p q c", q=Q, p=P)
    scratch = nc.dram_tensor("attn_scratch", (HALF, T, C), F32, kind="Internal").ap()
    scratch_t = scratch.rearrange("b (t q p) c -> b t p q c", q=Q, p=P)

    with ExitStack() as ctx:
        def sb(name, shape, dt=F32):
            return ctx.enter_context(nc.sbuf_tensor(name, shape, dt))

        def sem(name):
            return ctx.enter_context(nc.semaphore(name))

        names = ["k", "v", "r", "o"]
        WH = {n: sb(f"w{n}_hi", [P, CH, C], F32R) for n in names}
        WL = {n: sb(f"w{n}_lo", [P, CH, C], F32R) for n in names}
        WQ = sb("w_ternary", [P, CH, C], F32R)
        X = [sb(f"x{t}", [P, Q, C]) for t in range(2)]
        XN = sb("normed", [P, Q, C])
        ZA = sb("other", [P, Q, C])
        ZB = sb("parked", [P, Q, C])
        U = sb("evacuated", [P, 2, TILE])
        WS = sb("shifted_part", [P, 2, TILE])
        XH = [sb(f"xm_hi{t}", [P, CH, TILE], F32R) for t in range(2)]
        XL = [sb(f"xm_lo{t}", [P, CH, TILE], F32R) for t in range(2)]
        AH = sb("ffn_hi", [P, CH, TILE], F32R)
        AL = sb("ffn_lo", [P, CH, TILE], F32R)
        KV = sb("k_and_kv", [P, 2, 2, TILE])
        E = sb("gate", [P, 2, TILE])
        S = sb("scans", [P, 2, TILE + 1])
        RH = sb("rwkv_hi", [P, CH, TILE], F32R)
        RL = sb("rwkv_lo", [P, CH, TILE], F32R)
        ident = sb("ident", [P, P])
        tmx = sb("time_mix", [P, CH])
        tmx1 = sb("one_minus_mix", [P, CH])
        decay = sb("decay", [P, CH])
        first = sb("first", [P, CH])
        gam = sb("gamma_in", [P, CH])
        bet = sb("beta_in", [P, CH])
        gamq = sb("gamma_scaled", [P, CH])
        betq = sb("beta_scaled", [P, CH])
        state = sb("state", [P, CH, 2])
        last_x = sb("last_token", [P, CH])
        bnst = sb("bn_stats", [P, Q, 6])
        mv = sb("mean_var", [P, 2, Q, 2])
        half_neg = sb("minus_half", [P, Q])
        st = sb("stat_work", [P, 6, Q])
        own = sb("own_stats", [P, 2, 4, Q])
        oth = sb("other_stats", [P, 4, Q])
        am = sb("absmax", [P, 4 * CH])
        mx = sb("absmax_all", [P, 4 * CH])
        sc = sb("scalars", [P, 8])
        eps_k = sb("k_eps", [P, 1])
        one_c = sb("one", [P, 1])

        KVR = ctx.enter_context(nc.psum_tensor("kvr", [P, 3, TILE], F32))
        OUT = ctx.enter_context(nc.psum_tensor("out_banks", [P, Q, C], F32))
        TB = ctx.enter_context(nc.psum_tensor("transposed", [P, TILE], F32))

        s_x = [sem(f"x_loaded{t}") for t in range(2)]
        s_xst = [sem(f"x_stored{t}") for t in range(2)]
        s_oth = sem("other_loaded")
        s_park = sem("parked_loaded")
        s_parkst = sem("parked_stored")
        s_w = [sem(f"w_loaded_{n}") for n in names + ["f"]]
        s_small = sem("small_loaded")
        pe_w = sem("pe_weights_transposed")
        pe_g = sem("pe_groups")
        pe_t = sem("pe_slots")
        pe_out = sem("pe_out_banks")
        pe_rw = sem("pe_rwkv_chunks_read")
        pe_ah = sem("pe_ffn_chunks_read")
        act_w = sem("act_w_hi")
        act_k = sem("act_exp_k")
        act_r = sem("act_exp_r")
        act_le = sem("act_ln_gate")
        act_ls = sem("act_ln_sums")
        act_y = sem("act_quotient")
        act_rh = sem("act_rwkv_hi")
        act_u = sem("act_evacuated")
        act_z = sem("act_ffn_affine")
        act_h = sem("act_hi")
        act_c = sem("act_constants")
        dve_c = sem("dve_constants")
        dve_w = sem("dve_w_lo")
        dve_q = sem("dve_quantise")
        dve_min = sem("dve_k_clamped")
        dve_kv = sem("dve_kv")
        dve_scan = sem("dve_scans")
        dve_sum = sem("dve_sums")
        dve_l = sem("dve_log_denominator")
        dve_rw = sem("dve_rwkv")
        dve_rl = sem("dve_rwkv_lo")
        dve_x = sem("dve_mixed_or_clipped")
        dve_lo = sem("dve_lo")
        dve_am = sem("dve_absmax")
        dve_mx = sem("dve_absmax_all")
        dve_bn = sem("dve_bn_stats")
        dve_mv = sem("dve_mean_var")
        dve_out = sem("dve_out_banks_added")
        dve_s = sem("dve_scalars")
        pool_id = sem("pool_ident")
        pool_step = sem("pool_steps")
        dve_past = sem("dve_past_wait")
        pool_past = sem("pool_past_wait")
        pool_xn = sem("pool_normed")
        pool_za = sem("pool_other_normed")
        pool_sum = sem("pool_weight_sum")
        pool_max = sem("pool_gamma")

        STEPS = 8
        CREDIT = 1
        RING = 2
        BANKS = 4

        def user(b, ph, n):
            if ph == "P":
                return n
            if ph == "A":
                return CH + USERS_A * b + (n - 8 if n < 12 else CH + n - 20)
            return CH + USERS_A * HALF + USERS_B * (b - HALF) + n

        def uses_u(ph, n):
            return ph != "A" or SLOTS[n][0].startswith("mix")

        def am_count(b, n):
            return 4 * CH * b + sum(not k.startswith("mix") for k, _ in SLOTS[:n + 1])

        def bank_use(b, ph, what):
            before = Q * BANK_USES[ph].index(what)
            if ph == "A":
                return 2 * Q * b + before
            return 2 * Q * HALF + 6 * Q * (b - HALF) + before

        def slot_at(g):
            return SLOTS_AT.get(g)

        SLOTS_AT = {g: g for g in range(24)}

        weight_banks = [OUT[:, i, :] for i in range(4)] + [KVR[:, i, :] for i in range(3)]
        RAW = {"k": ZB, "v": ZA, "r": X[1], "o": KV[:, :, :, :].rearrange("p a b n -> p (a b) n")}

        block = ctx.enter_context(nc.Block())

        @block.sync
        def _(sp):
            sp.dma_start(X[0][:, :, :], x_t[0, 0]).then_inc(s_x[0], 16)
            for i, (n, w) in enumerate(zip(names, (Wk, Wv, Wr, Wo))):
                raw = RAW[n]
                sp.dma_start(raw if n == "o" else raw[:, :, :],
                             w.rearrange("(i p) c -> p i c", p=P)).then_inc(s_w[i], 16)
            sp.wait_ge(pe_w, CH)
            sp.dma_start(ZB[:, :, :], Wf.rearrange("(i p) c -> p i c", p=P)).then_inc(s_w[4], 16)
            sp.wait_ge(pe_w, 2 * CH)
            sp.dma_start(ZA[:, :, :], x_t[HALF, 0]).then_inc(s_oth, 16)
            sp.wait_ge(pe_w, 3 * CH)
            sp.dma_start(X[1][:, :, :], x_t[0, 1]).then_inc(s_x[1], 16)

            def batch(b, ph, is_last=False):
                own_dst, own_b = (scratch_t, b) if ph == "A" else (out_t, b)
                sp.wait_ge(pe_t, CH + 24 * b + 8)
                sp.dma_start(ZA[:, :, :], x_t[(b + HALF) % B, 1]).then_inc(s_oth, 16)
                if ph == "B":
                    sp.wait_ge(dve_out, BANKS + bank_use(b, ph, "other0") + Q)
                    sp.dma_start(out_t[b - HALF, 0], ZB[:, :, :]).then_inc(s_parkst, 16)
                    sp.wait_ge(s_parkst, 32 * (b - HALF) + 16)
                    sp.dma_start(ZB[:, :, :], scratch_t[b - HALF, 1]).then_inc(s_park, 16)
                sp.wait_ge(dve_out, BANKS + bank_use(b, ph, "attn0") + Q)
                sp.dma_start(own_dst[own_b, 0], X[0][:, :, :]).then_inc(s_xst[0], 16)
                sp.wait_ge(s_xst[0], 16 * b + 16)
                if not is_last:
                    sp.dma_start(X[0][:, :, :], x_t[b + 1, 0]).then_inc(s_x[0], 16)
                    sp.wait_ge(pe_t, CH + 24 * b + 20)
                    sp.dma_start(ZA[:, :, :], x_t[(b + HALF + 1) % B, 0]).then_inc(s_oth, 16)
                if ph == "B":
                    sp.wait_ge(dve_out, BANKS + bank_use(b, ph, "other1") + Q)
                    sp.dma_start(out_t[b - HALF, 1], ZB[:, :, :]).then_inc(s_parkst, 16)
                sp.wait_ge(dve_out, BANKS + bank_use(b, ph, "attn1") + Q)
                sp.dma_start(own_dst[own_b, 1], X[1][:, :, :]).then_inc(s_xst[1], 16)
                if ph == "B":
                    sp.wait_ge(s_parkst, 32 * (b - HALF) + 32)
                    if not is_last:
                        sp.dma_start(ZB[:, :, :], scratch_t[b - HALF + 1, 0]).then_inc(s_park, 16)
                sp.wait_ge(s_xst[1], 16 * b + 16)
                if not is_last:
                    sp.dma_start(X[1][:, :, :], x_t[b + 1, 1]).then_inc(s_x[1], 16)

            with sp.Fori(0, HALF) as b:
                batch(b, "A")
            sp.wait_ge(dve_q, 5)
            sp.dma_start(ZB[:, :, :], scratch_t[0, 0]).then_inc(s_park, 16)
            with sp.Fori(HALF, B - 1) as b:
                batch(b, "B")
            batch(B - 1, "B", is_last=True)

        @block.tensor
        def _(pe):
            pe.sem_inc(pe_g, CREDIT)
            pe.sem_inc(pe_rw, BANKS - 1)
            pe.sem_inc(pe_ah, BANKS - 1)

            def transpose_slot(b, ph, n, src):
                _, ch = SLOTS[n] if ph != "P" else ("mix_next0", n)
                for q in range(Q):
                    last = nc.tensor.transpose(TB[:, q * P:(q + 1) * P], src[:, q, ch * P:(ch + 1) * P],
                                               ident[:, :])
                last.then_inc(pe_t, 1)

            pe.wait_ge(pool_id, 2)
            unit = 0
            for i, n in enumerate(names):
                if i == 1:
                    pe.wait_ge(pool_xn, 1)
                    for m in range(CH):
                        if m:
                            pe.wait_ge(act_u, m)
                        transpose_slot(0, "P", m, XN)
                pe.wait_ge(s_w[i], 16)
                for ch in range(CH):
                    if unit >= len(weight_banks):
                        pe.wait_ge(dve_w, unit - len(weight_banks) + 1)
                    bank = weight_banks[unit % len(weight_banks)]
                    for j in range(C // P):
                        last = nc.tensor.transpose(bank[:, j * P:(j + 1) * P],
                                                   RAW[n][:, j, ch * P:(ch + 1) * P], ident[:, :])
                    last.then_inc(pe_w, 1)
                    unit += 1
            pe.wait_ge(dve_w, unit)

            def slot(b, ph, n):
                kind, _ = SLOTS[n]
                if n == 0:
                    pe.wait_ge(act_u, user(b, ph, 0) if ph == "B" else CH + USERS_A * b)
                elif uses_u(ph, n - 1):
                    pe.wait_ge(act_u, user(b, ph, n - 1) + 1)
                else:
                    pe.wait_ge(dve_am, am_count(b, n - 1))
                if n % CH == 0:
                    if "other" in kind:
                        pe.wait_ge(pool_za, 2 * b + int(kind[-1]) + 1)
                    else:
                        order = ["ffn_own0", "mix_own1", "ffn_own1", "mix_next0"].index(kind)
                        pe.wait_ge(pool_xn, 4 * b + order + 2)
                transpose_slot(b, ph, n, ZA if "other" in kind else XN)

            def project(b, ph, g):
                c, m = divmod(g, 3)
                t, j = divmod(c, CH)
                w = names[m]
                pe.wait_ge((act_k, dve_kv, act_r)[m], CREDIT + 8 * b + c)
                for ch in range(CH):
                    if j == 0 and m == 0:
                        if t == 1:
                            pe.wait_ge(dve_lo, RING + user(b, ph, 8 + ch) + 1)
                        elif ph == "A":
                            pe.wait_ge(dve_lo, RING + USERS_A * b + ch + 1)
                        else:
                            pe.wait_ge(dve_lo, RING + user(b, ph, 0) - CH + ch + 1)
                    hi = WH[w][:, ch, j * P:(j + 1) * P]
                    lo = WL[w][:, ch, j * P:(j + 1) * P]
                    nc.tensor.matmul(KVR[:, m, :], hi, XH[t][:, ch, :], start=(ch == 0), stop=False)
                    nc.tensor.matmul(KVR[:, m, :], hi, XL[t][:, ch, :], start=False, stop=False)
                    last = nc.tensor.matmul(KVR[:, m, :], lo, XH[t][:, ch, :], start=False, stop=(ch == CH - 1))
                last.then_inc(pe_g, 1)

            def attn_out(b, ph, t, slots=()):
                first_bank = bank_use(b, ph, f"attn{t}")
                for j in range(CH):
                    if j < len(slots):
                        slot(b, ph, slots[j])
                    pe.wait_ge(dve_rl, RING + 8 * b + 4 * t + j + 1)
                    for q in range(Q):
                        if j == 0:
                            pe.wait_ge(dve_out, first_bank + q + 1)
                        hi, lo = (r[:, j, q * P:(q + 1) * P] for r in (RH, RL))
                        nc.tensor.matmul(OUT[:, q, :], hi, WH["o"][:, j, :], start=(j == 0), stop=False)
                        nc.tensor.matmul(OUT[:, q, :], hi, WL["o"][:, j, :], start=False, stop=False)
                        last = nc.tensor.matmul(OUT[:, q, :], lo, WH["o"][:, j, :], start=False,
                                                stop=(j == CH - 1))
                        if j == CH - 1:
                            last.then_inc(pe_out, 1)
                    if j < CH - 1:
                        last.then_inc(pe_rw, 1)

            def ffn_out(b, what):
                first_bank = bank_use(b, "B", what)
                start_slot = {"own0": 0, "other0": 4, "own1": 12, "other1": 16}[what]
                for ch in range(CH):
                    pe.wait_ge(dve_lo, RING + user(b, "B", start_slot + ch) + 1)
                    for q in range(Q):
                        if ch == 0:
                            pe.wait_ge(dve_out, first_bank + q + 1)
                        nc.tensor.matmul(OUT[:, q, :], AH[:, ch, q * P:(q + 1) * P], WQ[:, ch, :],
                                         start=(ch == 0), stop=False)
                        last = nc.tensor.matmul(OUT[:, q, :], AL[:, ch, q * P:(q + 1) * P], WQ[:, ch, :],
                                                start=False, stop=(ch == CH - 1))
                        if ch == CH - 1:
                            last.then_inc(pe_out, 1)
                    if ch < CH - 1:
                        last.then_inc(pe_ah, 1)

            def batch(b, ph, is_last=False):
                for g in range(GROUPS):
                    n = slot_at(g)
                    if n is not None and not (is_last and n >= 20):
                        slot(b, ph, n)
                    project(b, ph, g)
                    if ph == "B" and g in FFN_AFTER:
                        ffn_out(b, FFN_AFTER[g])
                    if g == ATTN0_AFTER:
                        attn_out(b, ph, 0)
                attn_out(b, ph, 1)

            with pe.Fori(0, HALF) as b:
                batch(b, "A")
            pe.wait_ge(dve_q, 5)
            with pe.Fori(HALF, B - 1) as b:
                batch(b, "B")
            batch(B - 1, "B", is_last=True)

        @block.scalar
        def _(act):
            nc.scalar.preload_act_table_set("natural_log_exp_and_others")
            act.sem_inc(act_k, CREDIT)
            act.sem_inc(act_r, CREDIT)
            for dst, src in ((tmx, time_mix.rearrange("a b (j p) -> p (a b j)", p=P)),
                             (gam, ln_gamma.rearrange("(j p) -> p j", p=P)),
                             (bet, ln_beta.rearrange("(j p) -> p j", p=P))):
                act.dma_start(dst[:, :], src, allow_slow_non_contiguous=True).then_inc(s_small, 16)
            for g in range(HPC):
                for dst, src in ((decay, time_decay), (first, time_first)):
                    heads = src.rearrange("(j g) o -> g (o j)", g=HPC)[g:g + 1, :]
                    act.dma_start(dst[g * D:(g + 1) * D, :], heads.broadcast_to([D, CH]),
                                  allow_slow_non_contiguous=True).then_inc(s_small, 16)
            n_small = 16 * (3 + 2 * HPC)
            act.wait_ge(s_small, n_small)
            nc.scalar.activation(first[:, :], first[:, :], ACT.Exp).then_inc(act_c, 1)
            nc.scalar.activation(decay[:, :], decay[:, :], ACT.Exp).then_inc(act_c, 1)
            act.wait_ge(act_c, 2)
            nc.scalar.activation(decay[:, :], decay[:, :], ACT.Exp, scale=-1.0).then_inc(act_c, 1)

            def evacuate(b, ph, n):
                kind, ch = SLOTS[n] if ph != "P" else ("mix_next0", n)
                act.wait_ge(pe_t, (n if ph == "P" else CH + 24 * b + n) + 1)
                if not uses_u(ph, n):
                    nc.scalar.activation(TB[:, :], TB[:, :], ACT.Identity, bias=bet[:, ch:ch + 1],
                                         scale=gam[:, ch:ch + 1]).then_inc(act_z, 1)
                    return
                m = user(b, ph, n)
                act.wait_ge(dve_lo, m + 1)
                r = n % 2
                if kind.startswith("mix"):
                    nc.scalar.activation(U[:, r, :], TB[:, :], ACT.Copy, scale=tmx[:, ch:ch + 1])
                    nc.scalar.activation(WS[:, r, :], TB[:, :], ACT.Copy,
                                         scale=tmx1[:, ch:ch + 1]).then_inc(act_u, 1)
                else:
                    nc.scalar.activation(U[:, r, :], TB[:, :], ACT.Identity, bias=betq[:, ch:ch + 1],
                                         scale=gamq[:, ch:ch + 1]).then_inc(act_u, 1)

            def high_part(b, ph, n):
                if not uses_u(ph, n):
                    return
                kind, ch = SLOTS[n] if ph != "P" else ("mix_next0", n)
                m = user(b, ph, n)
                act.wait_ge(dve_x, m + 1)
                if kind.startswith("mix"):
                    t = int(kind[-1])
                    if ph == "P":
                        pass
                    elif kind == "mix_own1":
                        act.wait_ge(pe_g, CREDIT + 24 * b)
                    else:
                        act.wait_ge(pe_g, CREDIT + 24 * b + 12)
                    dst = XH[t][:, ch, :]
                else:
                    f = 4 * (b - HALF) + ["ffn_own0", "ffn_other0", "ffn_own1", "ffn_other1"].index(kind)
                    if ch < CH - 1:
                        act.wait_ge(pe_ah, 3 * f + ch + 1)
                    else:
                        before = {"ffn_own0": "attn1", "ffn_other0": "own0", "ffn_own1": "attn0",
                                  "ffn_other1": "own1"}[kind]
                        if kind == "ffn_own0":
                            act.wait_ge(pe_out, bank_use(b, ph, "own0"))
                        else:
                            act.wait_ge(pe_out, bank_use(b, ph, before) + Q)
                    dst = AH[:, ch, :]
                nc.scalar.activation(dst, U[:, n % 2, :], ACT.Copy).then_inc(act_h, 1)

            act.wait_ge(dve_c, 2)
            unit = 0
            for i, n in enumerate(names):
                if i == 1:
                    for m in range(CH):
                        if m:
                            high_part(0, "P", m - 1)
                        evacuate(0, "P", m)
                    high_part(0, "P", CH - 1)
                for ch in range(CH):
                    act.wait_ge(pe_w, unit + 1)
                    nc.scalar.activation(WH[n][:, ch, :], weight_banks[unit % len(weight_banks)],
                                         ACT.Copy).then_inc(act_w, 1)
                    unit += 1

            def exp_k(b, c):
                act.wait_ge(pe_g, CREDIT + 24 * b + 3 * c + 1)
                act.wait_ge(dve_rl, 8 * b + c + 1)
                nc.scalar.activation(KV[:, c % 2, 0, :], KVR[:, 0, :], ACT.Exp).then_inc(act_k, 1)

            def exp_r(b, c):
                act.wait_ge(pe_g, CREDIT + 24 * b + 3 * c + 3)
                nc.scalar.activation(E[:, c % 2, :], KVR[:, 2, :], ACT.Exp, scale=-1.0).then_inc(act_r, 1)
                act.wait_ge(act_r, CREDIT + 8 * b + c + 1)
                nc.scalar.activation(E[:, c % 2, :], E[:, c % 2, :], ACT.Ln, bias=one_c[:, :]).then_inc(act_le, 1)

            def ln_sums(b, c):
                act.wait_ge(dve_sum, CREDIT + 8 * b + c + 1)
                nc.scalar.activation(KV[:, c % 2, 0, :], KV[:, c % 2, 0, :], ACT.Ln,
                                     bias=eps_k[:, :]).then_inc(act_ls, 1)

            def quotient(b, c):
                act.wait_ge(dve_l, 8 * b + c + 1)
                nc.scalar.activation(E[:, c % 2, :], E[:, c % 2, :], ACT.Exp, scale=-1.0).then_inc(act_y, 1)

            def rwkv_hi(b, ph, c):
                t, j = divmod(c, CH)
                act.wait_ge(dve_rw, 8 * b + c + 1)
                if j < CH - 1:
                    act.wait_ge(pe_rw, 3 * (2 * b + t) + j + 1)
                elif t == 1:
                    act.wait_ge(pe_out, bank_use(b, ph, "attn0") + Q)
                else:
                    act.wait_ge(pe_rw, 3 * (2 * b) + CH - 1)
                    if ph == "B":
                        act.wait_ge(pe_out, bank_use(b, ph, "own0"))
                nc.scalar.activation(RH[:, j, :], KV[:, c % 2, 1, :], ACT.Copy).then_inc(act_rh, 1)

            def batch(b, ph, is_last=False):
                done = []

                def slot(n):
                    if done:
                        high_part(b, ph, done[-1])
                    evacuate(b, ph, n)
                    done.append(n)

                for g in range(GROUPS):
                    c, m = divmod(g, 3)
                    n = slot_at(g)
                    if n is not None and not (is_last and n >= 20):
                        slot(n)
                    if g == 20:
                        high_part(b, ph, done[-1])
                        done.clear()
                    if m == 0:
                        exp_k(b, c)
                        if c:
                            ln_sums(b, c - 1)
                            if c == CH:
                                quotient(b, c - 1)
                                rwkv_hi(b, ph, c - 1)
                    elif m == 1 and c and c != CH:
                        quotient(b, c - 1)
                    elif m == 2:
                        if c and c != CH:
                            rwkv_hi(b, ph, c - 1)
                        exp_r(b, c)
                if not is_last:
                    high_part(b, ph, 23)
                ln_sums(b, 2 * CH - 1)
                quotient(b, 2 * CH - 1)
                rwkv_hi(b, ph, 2 * CH - 1)

            with act.Fori(0, HALF) as b:
                batch(b, "A")
            act.wait_ge(dve_s, 5)
            with act.Fori(HALF, B - 1) as b:
                batch(b, "B")
            batch(B - 1, "B", is_last=True)

        @block.vector
        def _(dve):
            V = nc.vector
            dve.sem_inc(dve_kv, CREDIT)
            dve.sem_inc(dve_sum, CREDIT)
            dve.sem_inc(dve_rl, RING)
            dve.sem_inc(dve_lo, RING)
            dve.sem_inc(dve_out, BANKS)
            V.memset(eps_k[:, :], K_EPS)
            V.memset(one_c[:, :], 1.0)
            V.memset(half_neg[:, :], -0.5).then_inc(dve_c, 1)
            V.memset(mx[:, :], 0.0).then_inc(dve_mx, 1)

            def stats(i, src):
                dve.wait_ge(pool_step, max(STEPS * i, 1) if isinstance(i, int) else STEPS * i)
                if not isinstance(i, int) or i >= 1:
                    dve.wait_ge(dve_mv, i)
                for q in range(Q):
                    last = V.bn_stats(bnst[:, q, :], src[:, q, :])
                last.then_inc(dve_bn, 1)
                dve.wait_ge(dve_bn, i + 1)
                dve.sem_inc(dve_past, 1)

            def stats_of(i, r, src):
                stats(i, src)
                for q in range(Q):
                    last = V.bn_aggr(mv[:, r, q, :], bnst[:, q, :])
                last.then_inc(dve_mv, 1)

            dve.wait_ge(s_x[0], 16)
            stats_of(0, 0, X[0])
            dve.wait_ge(s_small, 16 * (3 + 2 * HPC))
            V.tensor_scalar(tmx1[:, :], tmx[:, :], -1.0, 1.0, ALU.mult, ALU.add).then_inc(dve_c, 1)

            def mix_or_clip(b, ph, n):
                kind, ch = SLOTS[n] if ph != "P" else ("mix_next0", n)
                if not uses_u(ph, n):
                    col = CH * ["ffn_own0", "ffn_other0", "ffn_own1", "ffn_other1"].index(kind) + ch
                    dve.wait_ge(act_z, am_count(b, n))
                    if n == 0:
                        dve.wait_ge(dve_mx, b + 1)
                    V.tensor_reduce(am[:, col:col + 1], TB[:, :], AX.X, ALU.max,
                                    apply_absolute_value=True).then_inc(dve_am, 1)
                    return
                m = user(b, ph, n)
                r = n % 2
                dve.wait_ge(act_u, m + 1)
                if kind.startswith("mix"):
                    if kind.endswith("0"):
                        V.tensor_copy(last_x[:, ch:ch + 1], WS[:, r, TILE - 1:TILE])
                    else:
                        V.tensor_tensor(U[:, r, 0:1], U[:, r, 0:1], last_x[:, ch:ch + 1], ALU.add)
                    V.tensor_tensor(U[:, r, 1:TILE], U[:, r, 1:TILE], WS[:, r, 0:TILE - 1],
                                    ALU.add).then_inc(dve_x, 1)
                else:
                    V.tensor_scalar(U[:, r, :], U[:, r, :], QB - FFN_EPS, -QB + FFN_EPS, ALU.min,
                                    ALU.max).then_inc(dve_x, 1)

            def low_part(b, ph, n):
                if not uses_u(ph, n):
                    return
                kind, ch = SLOTS[n] if ph != "P" else ("mix_next0", n)
                dve.wait_ge(act_h, user(b, ph, n) + 1)
                if kind.startswith("mix"):
                    t = int(kind[-1])
                    hi, lo = XH[t][:, ch, :], XL[t][:, ch, :]
                else:
                    hi, lo = AH[:, ch, :], AL[:, ch, :]
                V.tensor_tensor(lo, U[:, n % 2, :], hi.bitcast(F32), ALU.subtract).then_inc(dve_lo, 1)

            unit = 0
            for i, n in enumerate(names):
                if i == 1:
                    for m in range(CH):
                        if m:
                            low_part(0, "P", m - 1)
                        mix_or_clip(0, "P", m)
                    low_part(0, "P", CH - 1)
                for ch in range(CH):
                    dve.wait_ge(act_w, unit + 1)
                    V.tensor_tensor(WL[n][:, ch, :], weight_banks[unit % len(weight_banks)],
                                    WH[n][:, ch, :].bitcast(F32), ALU.subtract).then_inc(dve_w, 1)
                    unit += 1

            dve.wait_ge(s_w[4], 16)
            V.tensor_reduce(sc[:, 0:1], ZB[:, :, :], AX.XY, ALU.add, apply_absolute_value=True).then_inc(dve_q, 1)
            dve.wait_ge(pool_sum, 1)
            V.tensor_scalar(sc[:, 2:3], sc[:, 1:2], 1.0 / (C * C), None, ALU.mult).then_inc(dve_s, 1)
            dve.wait_ge(dve_s, 1)
            V.tensor_scalar(sc[:, 3:4], sc[:, 2:3], FFN_EPS, None, ALU.add).then_inc(dve_s, 1)
            dve.wait_ge(dve_s, 2)
            V.reciprocal(sc[:, 4:5], sc[:, 3:4]).then_inc(dve_q, 1)
            dve.wait_ge(dve_q, 2)
            V.tensor_scalar(WQ[:, :, :], ZB[:, :, :], sc[:, 4:5], 0.5, ALU.mult, ALU.is_gt).then_inc(dve_q, 1)
            V.tensor_scalar(ZB[:, :, :], ZB[:, :, :], sc[:, 4:5], -0.5, ALU.mult, ALU.is_lt).then_inc(dve_q, 1)
            dve.wait_ge(dve_q, 4)
            V.tensor_tensor(WQ[:, :, :], WQ[:, :, :].bitcast(F32), ZB[:, :, :], ALU.subtract).then_inc(dve_q, 1)

            def clamp_k(b, c):
                dve.wait_ge(act_k, CREDIT + 8 * b + c + 1)
                V.tensor_scalar(KV[:, c % 2, 0, :], KV[:, c % 2, 0, :], math.exp(K_CLAMP), None,
                                ALU.min).then_inc(dve_min, 1)

            def recurrence(b, c):
                t, j = divmod(c, CH)
                kv = KV[:, c % 2]
                dve.wait_ge(pe_g, CREDIT + 24 * b + 3 * c + 2)
                dve.wait_ge(dve_min, 8 * b + c + 1)
                V.tensor_tensor(kv[:, 1, :], kv[:, 0, :], KVR[:, 1, :], ALU.mult).then_inc(dve_kv, 1)
                dve.wait_ge(dve_sum, CREDIT + 8 * b + c)
                if t == 0:
                    V.memset(S[:, :, 0:1], 0.0)
                else:
                    V.tensor_copy(S[:, :, 0:1], state[:, j, :].rearrange("p (a o) -> p a o", o=1))
                dec = decay[:, j:j + 1].to_broadcast([P, TILE])
                for i in range(2):
                    if i == 1:
                        dve.wait_ge(dve_kv, CREDIT + 8 * b + c + 1)
                    last = V.tensor_tensor_scan(S[:, i, 1:TILE + 1], dec, kv[:, i, :],
                                                0.0 if t == 0 else state[:, j, i:i + 1], ALU.mult, ALU.add)
                last.then_inc(dve_scan, 1)
                dve.wait_ge(dve_scan, 8 * b + c + 1)
                if t == 0:
                    V.tensor_copy(state[:, j, :].rearrange("p (a o) -> p a o", o=1), S[:, :, TILE:TILE + 1])
                V.scalar_tensor_tensor(kv, kv, first[:, j:j + 1], S[:, :, 0:TILE], ALU.mult,
                                       ALU.add).then_inc(dve_sum, 1)

            def denominator(b, c):
                dve.wait_ge(act_ls, 8 * b + c + 1)
                V.tensor_tensor(E[:, c % 2, :], E[:, c % 2, :], KV[:, c % 2, 0, :], ALU.add).then_inc(dve_l, 1)

            def rwkv(b, c):
                dve.wait_ge(act_y, 8 * b + c + 1)
                V.tensor_tensor(KV[:, c % 2, 1, :], KV[:, c % 2, 1, :], E[:, c % 2, :], ALU.mult).then_inc(dve_rw, 1)

            def rwkv_lo(b, c):
                dve.wait_ge(act_rh, 8 * b + c + 1)
                V.tensor_tensor(RL[:, c % CH, :], KV[:, c % 2, 1, :], RH[:, c % CH, :].bitcast(F32),
                                ALU.subtract).then_inc(dve_rl, 1)

            def add_out(b, ph, what):
                use = bank_use(b, ph, what)
                t = int(what[-1])
                if what.startswith("attn") or what.startswith("own"):
                    tile = X[t]
                    dve.wait_ge(pool_xn, 4 * b + (2 if t == 0 else 4))
                else:
                    tile = ZB
                    dve.wait_ge(s_park, 32 * (b - HALF) + 16 * t + 16)
                if ph == "B" and what.startswith("attn"):
                    dve.wait_ge(dve_out, BANKS + bank_use(b, ph, f"own{t}") + Q)
                for q in range(Q):
                    dve.wait_ge(pe_out, use + q + 1)
                    if what.startswith("attn"):
                        V.tensor_tensor(tile[:, q, :], tile[:, q, :], OUT[:, q, :], ALU.add).then_inc(dve_out, 1)
                    else:
                        V.scalar_tensor_tensor(tile[:, q, :], OUT[:, q, :], sc[:, 7:8], tile[:, q, :],
                                               ALU.mult, ALU.add).then_inc(dve_out, 1)

            ADD_AFTER = {6: "own0", 10: "other0", 18: "own1", 22: "other1"}

            def batch(b, ph, is_last=False):
                done = []

                def slot(n):
                    if done:
                        low_part(b, ph, done[-1])
                    mix_or_clip(b, ph, n)
                    done.append(n)

                for g in range(GROUPS):
                    c, m = divmod(g, 3)
                    if g == 0:
                        dve.wait_ge(s_oth, 32 * b + 16)
                        stats_of(4 * b + 1, 1, ZA)
                    if g == 6:
                        dve.wait_ge(s_x[1], 16 * b + 16)
                        stats_of(4 * b + 2, 0, X[1])
                    if g == 13:
                        dve.wait_ge(s_oth, 32 * b + 32)
                        stats_of(4 * b + 3, 1, ZA)
                    if g == 18 and not is_last:
                        dve.wait_ge(s_x[0], 16 * b + 32)
                        stats_of(4 * b + 4, 0, X[0])
                    n = slot_at(g)
                    if n is not None and not (is_last and n >= 20):
                        slot(n)
                    if g == 20:
                        low_part(b, ph, done[-1])
                        done.clear()
                    if m == 0:
                        clamp_k(b, c)
                        if c:
                            denominator(b, c - 1)
                            if c == CH:
                                rwkv(b, c - 1)
                                rwkv_lo(b, c - 1)
                                add_out(b, ph, "attn0")
                    elif m == 1:
                        if c and c != CH:
                            rwkv(b, c - 1)
                        recurrence(b, c)
                    elif m == 2 and c and c != CH:
                        rwkv_lo(b, c - 1)
                    if ph == "B" and g in ADD_AFTER:
                        add_out(b, ph, ADD_AFTER[g])
                if not is_last:
                    low_part(b, ph, 23)
                denominator(b, 2 * CH - 1)
                rwkv(b, 2 * CH - 1)
                rwkv_lo(b, 2 * CH - 1)
                add_out(b, ph, "attn1")
                if ph == "A":
                    dve.wait_ge(dve_am, 4 * CH * b + 4 * CH)
                    V.tensor_tensor(mx[:, :], mx[:, :], am[:, :], ALU.max).then_inc(dve_mx, 1)

            with dve.Fori(0, HALF) as b:
                batch(b, "A")
            dve.wait_ge(dve_mx, HALF + 1)
            V.tensor_reduce(sc[:, 5:6], mx[:, :], AX.X, ALU.max).then_inc(dve_s, 1)
            dve.wait_ge(pool_max, 1)
            V.reciprocal(sc[:, 3:4], sc[:, 6:7]).then_inc(dve_s, 1)
            V.scalar_tensor_tensor(sc[:, 7:8], sc[:, 6:7], 1.0 / QB, sc[:, 2:3], ALU.mult, ALU.mult)
            dve.wait_ge(dve_s, 4)
            V.tensor_scalar(gamq[:, :], gam[:, :], QB, sc[:, 3:4], ALU.mult, ALU.mult)
            V.tensor_scalar(betq[:, :], bet[:, :], QB, sc[:, 3:4], ALU.mult, ALU.mult).then_inc(dve_s, 1)
            dve.wait_ge(dve_s, 5)
            with dve.Fori(HALF, B - 1) as b:
                batch(b, "B")
            batch(B - 1, "B", is_last=True)

        @block.gpsimd
        def _(pool):
            G = nc.gpsimd
            pool.sem_inc(pool_step, STEPS)
            G.memset(ident[:, :], 0.0).then_inc(pool_id, 1)
            pool.wait_ge(pool_id, 1)
            G.affine_select(out=ident[:, :], in_=ident[:, :], compare_op=ALU.not_equal, fill=1.0, base=0,
                            pattern=[[-1, P]], channel_multiplier=1).then_inc(pool_id, 1)

            def scales(i, r, dst):
                mean, var = mv[:, r, :, 0], mv[:, r, :, 1]
                k = [0]

                def step(instruction):
                    k[0] += 1
                    instruction.then_inc(pool_step, 1)
                    pool.wait_ge(pool_step, STEPS + i * STEPS + k[0])
                    pool.sem_inc(pool_past, 1)

                pool.wait_ge(dve_mv, i + 1)
                pool.sem_inc(pool_past, 1)
                step(G.tensor_scalar(st[:, 0, :], var, 1.0, LN_EPS, ALU.mult, ALU.add))
                step(G.tensor_tensor(dst[:, 0, :], st[:, 0, :], half_neg[:, :], ALU.pow))
                step(G.tensor_tensor(st[:, 1, :], var, dst[:, 0, :], ALU.mult))
                step(G.tensor_tensor(st[:, 2, :], st[:, 1, :], dst[:, 0, :], ALU.mult))
                step(G.tensor_scalar(st[:, 3, :], st[:, 2, :], 1.0, FFN_LN_EPS, ALU.mult, ALU.add))
                step(G.tensor_tensor(st[:, 4, :], st[:, 3, :], half_neg[:, :], ALU.pow))
                G.tensor_scalar(st[:, 5, :], mean, -1.0, 0.0, ALU.mult, ALU.add)
                step(G.tensor_tensor(dst[:, 2, :], st[:, 4, :], dst[:, 0, :], ALU.mult))
                G.tensor_tensor(dst[:, 1, :], st[:, 5, :], dst[:, 0, :], ALU.mult)
                step(G.tensor_tensor(dst[:, 3, :], st[:, 5, :], dst[:, 2, :], ALU.mult))
                assert k[0] == STEPS
                return k

            def normalise(dst, src, stats, kind, done):
                pool.sem_inc(pool_past, 1)
                for q in range(Q):
                    last = G.tensor_scalar(dst[:, q, :], src[:, q, :], stats[:, 2 * kind, q:q + 1],
                                           stats[:, 2 * kind + 1, q:q + 1], ALU.mult, ALU.add)
                last.then_inc(done, 1)

            pool.wait_ge(dve_c, 1)
            scales(0, 0, own[:, 0])
            normalise(XN, X[0], own[:, 0], 0, pool_xn)
            pool.wait_ge(dve_q, 1)
            G.partition_all_reduce(sc[:, 1:2], sc[:, 0:1], P, bass.bass_isa.ReduceOp.add).then_inc(pool_sum, 1)

            def batch(b, ph, is_last=False):
                pool.wait_ge(pe_t, CH + 24 * b)
                normalise(XN, X[0], own[:, 0], 1, pool_xn)
                scales(4 * b + 1, 1, oth)
                normalise(ZA, ZA, oth, 1, pool_za)
                scales(4 * b + 2, 0, own[:, 1])
                pool.wait_ge(pe_t, CH + 24 * b + 4)
                normalise(XN, X[1], own[:, 1], 0, pool_xn)
                pool.wait_ge(pe_t, CH + 24 * b + 12)
                normalise(XN, X[1], own[:, 1], 1, pool_xn)
                scales(4 * b + 3, 1, oth)
                normalise(ZA, ZA, oth, 1, pool_za)
                if not is_last:
                    scales(4 * b + 4, 0, own[:, 0])
                    pool.wait_ge(pe_t, CH + 24 * b + 16)
                    normalise(XN, X[0], own[:, 0], 0, pool_xn)

            with pool.Fori(0, HALF) as b:
                batch(b, "A")
            pool.wait_ge(dve_s, 3)
            G.partition_all_reduce(sc[:, 6:7], sc[:, 5:6], P, bass.bass_isa.ReduceOp.max).then_inc(pool_max, 1)
            with pool.Fori(HALF, B - 1) as b:
                batch(b, "B")
            batch(B - 1, "B", is_last=True)


_INS = ["L0_attn_x", "L0_attn_time_decay", "L0_attn_time_first", "L0_attn_time_mix", "L0_attn_Wk",
        "L0_attn_Wv", "L0_attn_Wr", "L0_attn_Wo", "L0_ffn_weight", "L0_ffn_ln_gamma", "L0_ffn_ln_beta"]


def kernel(**inputs):
    import numpy as np
    import concourse.bacc as bacc
    from concourse.bass_utils import run_bass_kernel_spmd

    nc = bacc.Bacc("TRN2", target_bir_lowering=False, num_devices=1)
    arrays, args = {}, []
    for name in _INS:
        a = np.ascontiguousarray(inputs[name])
        arrays[f"in_{name}"] = a
        args.append(nc.dram_tensor(f"in_{name}", a.shape, mybir.dt.from_np(a.dtype), kind="ExternalInput").ap())
    shape = arrays["in_L0_attn_x"].shape
    result = nc.dram_tensor("out", shape, F32, kind="ExternalOutput").ap()
    mixed_decay_kernel(nc, *args, result)
    r = run_bass_kernel_spmd(nc, [arrays], core_ids=[0])
    return r.results[0]["out"]
```

```python
from contextlib import ExitStack
import math

import concourse.bass as bass
from concourse import mybir

F32 = mybir.dt.float32
F32R = mybir.dt.float32r
ALU = mybir.AluOpType
ACT = mybir.ActivationFunctionType
AX = mybir.AxisListType

P = 128
TILE = 512
LN_EPS = 1e-5
FFN_LN_EPS = 1e-3
FFN_EPS = 1e-5
QB = 128.0
K_CLAMP = 60.0
K_EPS = 1e-16
ROUND = 1.5 * 2.0 ** 23

SLOT_KINDS = ["ffn_own0", "ffn_other0", "mix_own1", "ffn_own1", "ffn_other1", "mix_next0"]
SLOTS = [(kind, ch) for kind in SLOT_KINDS for ch in range(4)]
STATS_ORDER = ["other0", "own1", "other1", "next0"]
FFN_AFTER = {4: "own0", 8: "other0", 16: "own1", 20: "other1"}
BANK_USES = {"A": ["attn0", "attn1"],
             "B": ["own0", "other0", "attn0", "own1", "other1", "attn1"]}
ATTN0_AFTER = 12


def mixed_decay_kernel(nc, x, time_decay, time_first, time_mix, Wk, Wv, Wr, Wo, Wf, ln_gamma, ln_beta, out):
    B, T, C = x.shape
    H = time_decay.shape[0]
    CH = C // P
    Q = TILE // P
    D = C // H
    HPC = P // D
    HALF = B // 2
    assert (CH, Q, T // TILE, 2 * HALF) == (4, 4, 2, B)
    GROUPS = 2 * CH * 3

    x_t = x.rearrange("b (t q p) c -> b t p q c", q=Q, p=P)
    out_t = out.rearrange("b (t q p) c -> b t p q c", q=Q, p=P)
    scratch = nc.dram_tensor("attn_scratch", (HALF, T, C), F32, kind="Internal").ap()
    scratch_t = scratch.rearrange("b (t q p) c -> b t p q c", q=Q, p=P)

    with ExitStack() as ctx:
        def sb(name, shape, dt=F32):
            return ctx.enter_context(nc.sbuf_tensor(name, shape, dt))

        def sem(name):
            return ctx.enter_context(nc.semaphore(name))

        names = ["k", "v", "r", "o"]
        WH = {n: sb(f"w{n}_hi", [P, CH, C], F32R) for n in names}
        WL = {n: sb(f"w{n}_lo", [P, CH, C], F32R) for n in names}
        WQ = sb("w_ternary", [P, CH, C], F32R)
        X = [sb(f"x{t}", [P, Q, C]) for t in range(2)]
        XN = sb("normed", [P, Q, C])
        ZA = sb("other", [P, Q, C])
        ZB = sb("parked", [P, Q, C])
        U = sb("evacuated", [P, 2, TILE])
        WS = sb("shifted_part", [P, 2, TILE])
        XH = [sb(f"xm_hi{t}", [P, CH, TILE], F32R) for t in range(2)]
        XL = [sb(f"xm_lo{t}", [P, CH, TILE], F32R) for t in range(2)]
        AH = sb("ffn_hi", [P, CH, TILE], F32R)
        AL = sb("ffn_lo", [P, CH, TILE], F32R)
        KV = sb("k_and_kv", [P, 2, 2, TILE])
        E = sb("gate", [P, 2, TILE])
        S = sb("scans", [P, 2, TILE + 1])
        RH = sb("rwkv_hi", [P, CH, TILE], F32R)
        RL = sb("rwkv_lo", [P, CH, TILE], F32R)
        ident = sb("ident", [P, P])
        tmx = sb("time_mix", [P, CH])
        tmx1 = sb("one_minus_mix", [P, CH])
        decay = sb("decay", [P, CH])
        first = sb("first", [P, CH])
        gam = sb("gamma_in", [P, CH])
        bet = sb("beta_in", [P, CH])
        gamq = sb("gamma_scaled", [P, CH])
        betq = sb("beta_scaled", [P, CH])
        state = sb("state", [P, CH, 2])
        last_x = sb("last_token", [P, CH])
        bnst = sb("bn_stats", [P, Q, 6])
        mv = sb("mean_var", [P, 2, Q, 2])
        half_neg = sb("minus_half", [P, Q])
        st = sb("stat_work", [P, 6, Q])
        own = sb("own_stats", [P, 2, 4, Q])
        oth = sb("other_stats", [P, 4, Q])
        am = sb("absmax", [P, 4 * CH])
        mx = sb("absmax_all", [P, 4 * CH])
        rows = sb("rows", [3 * CH, P])
        heads = sb("heads", [2 * CH, HPC])
        head_rows = sb("head_rows", [2 * CH, P])
        sc = sb("scalars", [P, 8])
        eps_k = sb("k_eps", [P, 1])
        round_c = sb("minus_round", [P, 1])
        one_c = sb("one", [P, 1])

        KVR = ctx.enter_context(nc.psum_tensor("kvr", [P, 3, TILE], F32))
        OUT = ctx.enter_context(nc.psum_tensor("out_banks", [P, Q, C], F32))
        TB = ctx.enter_context(nc.psum_tensor("transposed", [P, TILE], F32))

        s_x = [sem(f"x_loaded{t}") for t in range(2)]
        s_xst = [sem(f"x_stored{t}") for t in range(2)]
        s_oth = sem("other_loaded")
        s_park = sem("parked_loaded")
        s_parkst = sem("parked_stored")
        s_w = [sem(f"w_loaded_{n}") for n in names + ["f"]]
        s_small = sem("small_loaded")
        pe_w = sem("pe_weights_transposed")
        pe_g = sem("pe_groups")
        pe_t = sem("pe_slots")
        pe_out = sem("pe_out_banks")
        pe_rw = sem("pe_rwkv_chunks_read")
        pe_ah = sem("pe_ffn_chunks_read")
        pe_c = sem("pe_constants_transposed")
        act_w = sem("act_w_hi")
        act_k = sem("act_exp_k")
        act_r = sem("act_exp_r")
        act_q = sem("act_ternary")
        act_le = sem("act_ln_gate")
        act_ls = sem("act_ln_sums")
        act_y = sem("act_quotient")
        act_rh = sem("act_rwkv_hi")
        act_u = sem("act_evacuated")
        act_h = sem("act_hi")
        act_c = sem("act_constants")
        dve_c = sem("dve_constants")
        dve_w = sem("dve_w_lo")
        dve_q = sem("dve_quantise")
        dve_min = sem("dve_k_clamped")
        dve_kv = sem("dve_kv")
        dve_scan = sem("dve_scans")
        dve_sum = sem("dve_sums")
        dve_l = sem("dve_log_denominator")
        dve_rw = sem("dve_rwkv")
        dve_rl = sem("dve_rwkv_lo")
        dve_x = sem("dve_mixed_or_clipped")
        dve_lo = sem("dve_lo")
        dve_mx = sem("dve_absmax_all")
        dve_bn = sem("dve_bn_stats")
        dve_mv = sem("dve_mean_var")
        dve_out = sem("dve_out_banks_added")
        dve_s = sem("dve_scalars")
        pool_id = sem("pool_ident")
        pool_step = sem("pool_steps")
        dve_past = sem("dve_past_wait")
        pool_past = sem("pool_past_wait")
        pool_xn = sem("pool_normed")
        pool_za = sem("pool_other_normed")
        pool_sum = sem("pool_weight_sum")
        pool_max = sem("pool_gamma")

        STEPS = 8
        CREDIT = 1
        RING = 2
        BANKS = 4

        def slots_before(b, ph, n):
            return n if ph == "P" else CH + len(SLOTS) * b + n

        def splits_before(b, ph, n):
            if ph == "P":
                return n
            if ph == "A":
                return CH + 2 * CH * b + sum(kind.startswith("mix") for kind, _ in SLOTS[:n])
            return CH + 2 * CH * HALF + len(SLOTS) * (b - HALF) + n

        def is_split(ph, n):
            return ph != "A" or SLOTS[n][0].startswith("mix")

        def slot_of(ph, n):
            return ("mix_next0", n) if ph == "P" else SLOTS[n]

        def first_slot(kind):
            return SLOTS.index((kind, 0))

        def normed_count(b, kind):
            return 1 + 4 * b + [k for k in SLOT_KINDS if "other" not in k].index(kind) + 1

        def stats_number(b, tile):
            return 4 * b + STATS_ORDER.index(tile) + 1

        def bank_use(b, ph, what):
            before = Q * BANK_USES[ph].index(what)
            if ph == "A":
                return 2 * Q * b + before
            return 2 * Q * HALF + 6 * Q * (b - HALF) + before

        def slot_ahead(g, is_last):
            return None if is_last and SLOTS[g][0] == "mix_next0" else g

        weight_banks = [OUT[:, i, :] for i in range(Q)]
        first_banks = [TB[:, :]] + [KVR[:, i, :] for i in range(3)]
        PROLOGUE = ["k", "v", "r", "slots", "o"]

        RAW = {"k": ZB, "v": ZA, "r": X[1], "o": KV[:, :, :, :].rearrange("p a b n -> p (a b) n")}

        block = ctx.enter_context(nc.Block())

        @block.sync
        def _(sp):
            for i, src in enumerate((time_mix.rearrange("a b (j p) -> (a b j) p", p=P),
                                     ln_gamma.rearrange("(j p) -> j p", p=P),
                                     ln_beta.rearrange("(j p) -> j p", p=P))):
                sp.dma_start(rows[i * CH:(i + 1) * CH, :], src).then_inc(s_small, 16)
            for i, src in enumerate((time_decay, time_first)):
                sp.dma_start(heads[i * CH:(i + 1) * CH, :],
                              src.rearrange("(j g) o -> j (g o)", g=HPC)).then_inc(s_small, 16)
            sp.dma_start(X[0][:, :, :], x_t[0, 0]).then_inc(s_x[0], 16)
            for i, (n, w) in enumerate(zip(names, (Wk, Wv, Wr, Wo))):
                raw = RAW[n]
                sp.dma_start(raw if n == "o" else raw[:, :, :],
                             w.rearrange("(i p) c -> p i c", p=P)).then_inc(s_w[i], 16)
            sp.wait_ge(pe_w, CH)
            sp.dma_start(ZB[:, :, :], Wf.rearrange("(i p) c -> p i c", p=P)).then_inc(s_w[4], 16)
            sp.wait_ge(pe_w, 2 * CH)
            sp.dma_start(ZA[:, :, :], x_t[HALF, 0]).then_inc(s_oth, 16)
            sp.wait_ge(pe_w, 3 * CH)
            sp.dma_start(X[1][:, :, :], x_t[0, 1]).then_inc(s_x[1], 16)

            def batch(b, ph, is_last=False):
                own_dst, own_b = (scratch_t, b) if ph == "A" else (out_t, b)
                sp.wait_ge(pe_t, slots_before(b, ph, first_slot("ffn_other0") + CH))
                sp.dma_start(ZA[:, :, :], x_t[(b + HALF) % B, 1]).then_inc(s_oth, 16)
                if ph == "B":
                    sp.wait_ge(dve_out, BANKS + bank_use(b, ph, "other0") + Q)
                    sp.dma_start(out_t[b - HALF, 0], ZB[:, :, :]).then_inc(s_parkst, 16)
                    sp.wait_ge(s_parkst, 32 * (b - HALF) + 16)
                    sp.dma_start(ZB[:, :, :], scratch_t[b - HALF, 1]).then_inc(s_park, 16)
                sp.wait_ge(dve_out, BANKS + bank_use(b, ph, "attn0") + Q)
                sp.dma_start(own_dst[own_b, 0], X[0][:, :, :]).then_inc(s_xst[0], 16)
                sp.wait_ge(s_xst[0], 16 * b + 16)
                if not is_last:
                    sp.dma_start(X[0][:, :, :], x_t[b + 1, 0]).then_inc(s_x[0], 16)
                    sp.wait_ge(pe_t, slots_before(b, ph, first_slot("ffn_other1") + CH))
                    sp.dma_start(ZA[:, :, :], x_t[(b + HALF + 1) % B, 0]).then_inc(s_oth, 16)
                if ph == "B":
                    sp.wait_ge(dve_out, BANKS + bank_use(b, ph, "other1") + Q)
                    sp.dma_start(out_t[b - HALF, 1], ZB[:, :, :]).then_inc(s_parkst, 16)
                sp.wait_ge(dve_out, BANKS + bank_use(b, ph, "attn1") + Q)
                sp.dma_start(own_dst[own_b, 1], X[1][:, :, :]).then_inc(s_xst[1], 16)
                if ph == "B":
                    sp.wait_ge(s_parkst, 32 * (b - HALF) + 32)
                    if not is_last:
                        sp.dma_start(ZB[:, :, :], scratch_t[b - HALF + 1, 0]).then_inc(s_park, 16)
                sp.wait_ge(s_xst[1], 16 * b + 16)
                if not is_last:
                    sp.dma_start(X[1][:, :, :], x_t[b + 1, 1]).then_inc(s_x[1], 16)

            with sp.Fori(0, HALF) as b:
                batch(b, "A")
            sp.wait_ge(act_q, 1)
            sp.dma_start(ZB[:, :, :], scratch_t[0, 0]).then_inc(s_park, 16)
            with sp.Fori(HALF, B - 1) as b:
                batch(b, "B")
            batch(B - 1, "B", is_last=True)

        @block.tensor
        def _(pe):
            pe.sem_inc(pe_g, CREDIT)
            pe.sem_inc(pe_rw, BANKS - 1)
            pe.sem_inc(pe_ah, BANKS - 1)

            def transpose_slot(b, ph, n, src):
                _, ch = slot_of(ph, n)
                bank = first_banks[n] if ph == "P" else TB[:, :]
                for q in range(Q):
                    last = nc.tensor.transpose(bank[:, q * P:(q + 1) * P], src[:, q, ch * P:(ch + 1) * P],
                                               ident[:, :])
                last.then_inc(pe_t, 1)

            pe.wait_ge(pool_id, 2)
            pe.wait_ge(s_small, 16 * 5)
            nc.tensor.transpose(TB[:, 0:3 * CH], rows[:, :], ident[0:3 * CH, 0:3 * CH]).then_inc(pe_c, 1)
            pe.wait_ge(dve_c, 2)
            nc.tensor.transpose(TB[:, 3 * CH:5 * CH], head_rows[:, :], ident[0:2 * CH, 0:2 * CH]).then_inc(pe_c, 1)
            unit = 0
            for n in PROLOGUE:
                if n == "slots":
                    pe.wait_ge(pool_xn, 1)
                    pe.wait_ge(dve_c, 3)
                    for m in range(CH):
                        transpose_slot(0, "P", m, XN)
                    continue
                pe.wait_ge(s_w[names.index(n)], 16)
                for ch in range(CH):
                    if unit >= len(weight_banks):
                        pe.wait_ge(dve_w, unit - len(weight_banks) + 1)
                    bank = weight_banks[unit % len(weight_banks)]
                    for j in range(C // P):
                        last = nc.tensor.transpose(bank[:, j * P:(j + 1) * P],
                                                   RAW[n][:, j, ch * P:(ch + 1) * P], ident[:, :])
                    last.then_inc(pe_w, 1)
                    unit += 1
            pe.wait_ge(dve_w, 3 * CH)
            pe.wait_ge(act_u, CH)

            def slot(b, ph, n):
                kind, _ = slot_of(ph, n)
                pe.wait_ge(act_u, slots_before(b, ph, n))
                if n % CH == 0:
                    if "other" in kind:
                        pe.wait_ge(pool_za, 2 * b + int(kind[-1]) + 1)
                    else:
                        pe.wait_ge(pool_xn, normed_count(b, kind))
                transpose_slot(b, ph, n, ZA if "other" in kind else XN)

            def project(b, ph, g):
                c, m = divmod(g, 3)
                t, j = divmod(c, CH)
                w = names[m]
                pe.wait_ge((act_k, dve_kv, act_r)[m], CREDIT + 8 * b + c)
                for ch in range(CH):
                    if j == 0 and m == 0:
                        slot0 = first_slot("mix_own1") if t == 1 else -CH
                        pe.wait_ge(dve_lo, RING + slots_before(b, ph, slot0 + ch) + 1)
                    hi = WH[w][:, ch, j * P:(j + 1) * P]
                    lo = WL[w][:, ch, j * P:(j + 1) * P]
                    nc.tensor.matmul(KVR[:, m, :], hi, XH[t][:, ch, :], start=(ch == 0), stop=False)
                    nc.tensor.matmul(KVR[:, m, :], hi, XL[t][:, ch, :], start=False, stop=False)
                    last = nc.tensor.matmul(KVR[:, m, :], lo, XH[t][:, ch, :], start=False, stop=(ch == CH - 1))
                last.then_inc(pe_g, 1)

            def attn_out(b, ph, t):
                first_bank = bank_use(b, ph, f"attn{t}")
                pe.wait_ge(dve_w, 4 * CH)
                for j in range(CH):
                    pe.wait_ge(dve_rl, RING + 8 * b + 4 * t + j + 1)
                    for q in range(Q):
                        if j == 0:
                            pe.wait_ge(dve_out, first_bank + q + 1)
                        hi, lo = (r[:, j, q * P:(q + 1) * P] for r in (RH, RL))
                        nc.tensor.matmul(OUT[:, q, :], hi, WH["o"][:, j, :], start=(j == 0), stop=False)
                        nc.tensor.matmul(OUT[:, q, :], hi, WL["o"][:, j, :], start=False, stop=False)
                        last = nc.tensor.matmul(OUT[:, q, :], lo, WH["o"][:, j, :], start=False,
                                                stop=(j == CH - 1))
                        if j == CH - 1:
                            last.then_inc(pe_out, 1)
                    if j < CH - 1:
                        last.then_inc(pe_rw, 1)

            def ffn_out(b, what):
                first_bank = bank_use(b, "B", what)
                start_slot = first_slot(f"ffn_{what}")
                for ch in range(CH):
                    pe.wait_ge(dve_lo, RING + slots_before(b, "any", start_slot + ch) + 1)
                    for q in range(Q):
                        if ch == 0:
                            pe.wait_ge(dve_out, first_bank + q + 1)
                        nc.tensor.matmul(OUT[:, q, :], AH[:, ch, q * P:(q + 1) * P], WQ[:, ch, :],
                                         start=(ch == 0), stop=False)
                        last = nc.tensor.matmul(OUT[:, q, :], AL[:, ch, q * P:(q + 1) * P], WQ[:, ch, :],
                                                start=False, stop=(ch == CH - 1))
                        if ch == CH - 1:
                            last.then_inc(pe_out, 1)
                    if ch < CH - 1:
                        last.then_inc(pe_ah, 1)

            def batch(b, ph, is_last=False):
                for g in range(GROUPS):
                    n = slot_ahead(g, is_last)
                    if n is not None:
                        slot(b, ph, n)
                    project(b, ph, g)
                    if ph == "B" and g in FFN_AFTER:
                        ffn_out(b, FFN_AFTER[g])
                    if g == ATTN0_AFTER:
                        attn_out(b, ph, 0)
                attn_out(b, ph, 1)

            with pe.Fori(0, HALF) as b:
                batch(b, "A")
            pe.wait_ge(act_q, 1)
            with pe.Fori(HALF, B - 1) as b:
                batch(b, "B")
            batch(B - 1, "B", is_last=True)

        @block.scalar
        def _(act):
            nc.scalar.preload_act_table_set("natural_log_exp_and_others")
            act.sem_inc(act_k, CREDIT)
            act.sem_inc(act_r, CREDIT)
            def evacuate(b, ph, n):
                kind, ch = slot_of(ph, n)
                bank = first_banks[n] if ph == "P" else TB[:, :]
                m = slots_before(b, ph, n)
                act.wait_ge(pe_t, m + 1)
                act.wait_ge(dve_lo, m + 1)
                r = n % 2
                if kind.startswith("mix"):
                    nc.scalar.activation(U[:, r, :], bank, ACT.Copy, scale=tmx[:, ch:ch + 1])
                    nc.scalar.activation(WS[:, r, :], bank, ACT.Copy,
                                         scale=tmx1[:, ch:ch + 1]).then_inc(act_u, 1)
                elif ph == "A":
                    nc.scalar.activation(U[:, r, :], bank, ACT.Identity, bias=bet[:, ch:ch + 1],
                                         scale=gam[:, ch:ch + 1]).then_inc(act_u, 1)
                else:
                    nc.scalar.activation(U[:, r, :], bank, ACT.Identity, bias=betq[:, ch:ch + 1],
                                         scale=gamq[:, ch:ch + 1]).then_inc(act_u, 1)

            def high_part(b, ph, n):
                kind, ch = slot_of(ph, n)
                if not is_split(ph, n):
                    return
                act.wait_ge(dve_x, splits_before(b, ph, n) + 1)
                if kind.startswith("mix"):
                    t = int(kind[-1])
                    if ph == "P":
                        pass
                    elif kind == "mix_own1":
                        act.wait_ge(pe_g, CREDIT + 24 * b)
                    else:
                        act.wait_ge(pe_g, CREDIT + 24 * b + 12)
                    dst = XH[t][:, ch, :]
                else:
                    f = 4 * (b - HALF) + ["ffn_own0", "ffn_other0", "ffn_own1", "ffn_other1"].index(kind)
                    if ch < CH - 1:
                        act.wait_ge(pe_ah, 3 * f + ch + 1)
                    else:
                        before = {"ffn_own0": "attn1", "ffn_other0": "own0", "ffn_own1": "attn0",
                                  "ffn_other1": "own1"}[kind]
                        if kind == "ffn_own0":
                            act.wait_ge(pe_out, bank_use(b, ph, "own0"))
                        else:
                            act.wait_ge(pe_out, bank_use(b, ph, before) + Q)
                    dst = AH[:, ch, :]
                nc.scalar.activation(dst, U[:, n % 2, :], ACT.Copy).then_inc(act_h, 1)

            unit = 0
            for n in PROLOGUE:
                if n == "slots":
                    act.wait_ge(dve_c, 4)
                    for pair in range(0, CH, 2):
                        for m in (pair, pair + 1):
                            evacuate(0, "P", m)
                        for m in (pair, pair + 1):
                            high_part(0, "P", m)
                    nc.scalar.activation(decay[:, :], decay[:, :], ACT.Exp, scale=-1.0).then_inc(act_c, 1)
                    continue
                for ch in range(CH):
                    act.wait_ge(pe_w, unit + 1)
                    nc.scalar.activation(WH[n][:, ch, :], weight_banks[unit % len(weight_banks)],
                                         ACT.Copy).then_inc(act_w, 1)
                    unit += 1
                if n == "k":
                    act.wait_ge(dve_c, 3)
                    nc.scalar.activation(first[:, :], first[:, :], ACT.Exp)
                    nc.scalar.activation(decay[:, :], decay[:, :], ACT.Exp).then_inc(act_c, 1)
                    act.wait_ge(act_c, 1)

            def exp_k(b, c):
                act.wait_ge(pe_g, CREDIT + 24 * b + 3 * c + 1)
                act.wait_ge(dve_rl, 8 * b + c + 1)
                nc.scalar.activation(KV[:, c % 2, 0, :], KVR[:, 0, :], ACT.Exp).then_inc(act_k, 1)

            def exp_r(b, c):
                act.wait_ge(pe_g, CREDIT + 24 * b + 3 * c + 3)
                nc.scalar.activation(E[:, c % 2, :], KVR[:, 2, :], ACT.Exp, scale=-1.0).then_inc(act_r, 1)
                act.wait_ge(act_r, CREDIT + 8 * b + c + 1)
                nc.scalar.activation(E[:, c % 2, :], E[:, c % 2, :], ACT.Ln, bias=one_c[:, :]).then_inc(act_le, 1)

            def ln_sums(b, c):
                act.wait_ge(dve_sum, CREDIT + 8 * b + c + 1)
                nc.scalar.activation(KV[:, c % 2, 0, :], KV[:, c % 2, 0, :], ACT.Ln,
                                     bias=eps_k[:, :]).then_inc(act_ls, 1)

            def quotient(b, c):
                act.wait_ge(dve_l, 8 * b + c + 1)
                nc.scalar.activation(E[:, c % 2, :], E[:, c % 2, :], ACT.Exp, scale=-1.0).then_inc(act_y, 1)

            def rwkv_hi(b, ph, c):
                t, j = divmod(c, CH)
                act.wait_ge(dve_rw, 8 * b + c + 1)
                if j < CH - 1:
                    act.wait_ge(pe_rw, 3 * (2 * b + t) + j + 1)
                elif t == 1:
                    act.wait_ge(pe_out, bank_use(b, ph, "attn0") + Q)
                else:
                    act.wait_ge(pe_rw, 3 * (2 * b) + CH - 1)
                    if ph == "B":
                        act.wait_ge(pe_out, bank_use(b, ph, "own0"))
                nc.scalar.activation(RH[:, j, :], KV[:, c % 2, 1, :], ACT.Copy).then_inc(act_rh, 1)

            def batch(b, ph, is_last=False):
                last = None
                for g in range(GROUPS):
                    c, m = divmod(g, 3)
                    n = slot_ahead(g, is_last)
                    if last is not None:
                        high_part(b, ph, last)
                    if n is not None:
                        evacuate(b, ph, n)
                    last = n
                    if m == 0:
                        exp_k(b, c)
                        if c:
                            ln_sums(b, c - 1)
                            if c == CH:
                                quotient(b, c - 1)
                                rwkv_hi(b, ph, c - 1)
                    elif m == 1 and c and c != CH:
                        quotient(b, c - 1)
                    elif m == 2:
                        if c and c != CH:
                            rwkv_hi(b, ph, c - 1)
                        exp_r(b, c)
                if last is not None:
                    high_part(b, ph, last)
                ln_sums(b, 2 * CH - 1)
                quotient(b, 2 * CH - 1)
                rwkv_hi(b, ph, 2 * CH - 1)

            with act.Fori(0, HALF) as b:
                batch(b, "A")
            act.wait_ge(dve_q, 3)
            nc.scalar.activation(WQ[:, :, :], ZB[:, :, :], ACT.Sign, bias=round_c[:, :]).then_inc(act_q, 1)
            act.wait_ge(dve_s, 5)
            with act.Fori(HALF, B - 1) as b:
                batch(b, "B")
            batch(B - 1, "B", is_last=True)

        @block.vector
        def _(dve):
            V = nc.vector
            dve.sem_inc(dve_kv, CREDIT)
            dve.sem_inc(dve_sum, CREDIT)
            dve.sem_inc(dve_rl, RING)
            dve.sem_inc(dve_lo, RING)
            dve.sem_inc(dve_out, BANKS)
            V.memset(eps_k[:, :], K_EPS)
            V.memset(round_c[:, :], -ROUND)
            V.memset(one_c[:, :], 1.0)
            V.memset(half_neg[:, :], -0.5).then_inc(dve_c, 1)
            V.memset(mx[:, :], 0.0).then_inc(dve_mx, 1)

            def stats(i, src):
                dve.wait_ge(pool_step, max(STEPS * i, 1) if isinstance(i, int) else STEPS * i)
                if not isinstance(i, int) or i >= 1:
                    dve.wait_ge(dve_mv, i)
                for q in range(Q):
                    last = V.bn_stats(bnst[:, q, :], src[:, q, :])
                last.then_inc(dve_bn, 1)
                dve.wait_ge(dve_bn, i + 1)
                dve.sem_inc(dve_past, 1)

            def stats_of(i, src, place):
                stats(i, src)
                for q in range(Q):
                    last = V.bn_aggr(mv[:, place, q, :], bnst[:, q, :])
                last.then_inc(dve_mv, 1)

            dve.wait_ge(s_small, 16 * 5)
            V.tensor_copy(head_rows[:, :].rearrange("j (g d) -> j g d", g=HPC),
                          heads[:, :].rearrange("j (g o) -> j g o", o=1).to_broadcast([2 * CH, HPC, D])
                          ).then_inc(dve_c, 1)
            dve.wait_ge(s_x[0], 16)
            stats_of(0, X[0], 0)
            dve.wait_ge(pe_c, 2)
            for i, dst in enumerate((tmx, gam, bet, decay, first)):
                last = V.tensor_copy(dst[:, :], TB[:, i * CH:(i + 1) * CH])
            last.then_inc(dve_c, 1)
            dve.wait_ge(dve_c, 3)
            V.tensor_scalar(tmx1[:, :], tmx[:, :], -1.0, 1.0, ALU.mult, ALU.add).then_inc(dve_c, 1)

            def mix_or_clip(b, ph, n):
                kind, ch = slot_of(ph, n)
                m = slots_before(b, ph, n)
                r = n % 2
                dve.wait_ge(act_u, m + 1)
                if kind.startswith("mix"):
                    if kind.endswith("0"):
                        V.tensor_copy(last_x[:, ch:ch + 1], WS[:, r, TILE - 1:TILE])
                    else:
                        V.tensor_tensor(U[:, r, 0:1], U[:, r, 0:1], last_x[:, ch:ch + 1], ALU.add)
                    V.tensor_tensor(U[:, r, 1:TILE], U[:, r, 1:TILE], WS[:, r, 0:TILE - 1],
                                    ALU.add).then_inc(dve_x, 1)
                elif ph == "A":
                    if n == 0:
                        dve.wait_ge(dve_mx, b + 1)
                    col = n if n < first_slot("mix_own1") else n - CH
                    V.tensor_reduce(am[:, col:col + 1], U[:, r, :], AX.X, ALU.max,
                                    apply_absolute_value=True).then_inc(dve_lo, 1)
                else:
                    V.tensor_scalar(U[:, r, :], U[:, r, :], QB - FFN_EPS, -QB + FFN_EPS, ALU.min,
                                    ALU.max).then_inc(dve_x, 1)

            def low_part(b, ph, n):
                kind, ch = slot_of(ph, n)
                if not is_split(ph, n):
                    return
                dve.wait_ge(act_h, splits_before(b, ph, n) + 1)
                if kind.startswith("mix"):
                    t = int(kind[-1])
                    hi, lo = XH[t][:, ch, :], XL[t][:, ch, :]
                else:
                    hi, lo = AH[:, ch, :], AL[:, ch, :]
                V.tensor_tensor(lo, U[:, n % 2, :], hi.bitcast(F32), ALU.subtract).then_inc(dve_lo, 1)

            unit = 0
            for n in PROLOGUE:
                if n == "slots":
                    for pair in range(0, CH, 2):
                        for m in (pair, pair + 1):
                            mix_or_clip(0, "P", m)
                        for m in (pair, pair + 1):
                            low_part(0, "P", m)
                    continue
                for ch in range(CH):
                    dve.wait_ge(act_w, unit + 1)
                    V.tensor_tensor(WL[n][:, ch, :], weight_banks[unit % len(weight_banks)],
                                    WH[n][:, ch, :].bitcast(F32), ALU.subtract).then_inc(dve_w, 1)
                    unit += 1

            dve.wait_ge(s_w[4], 16)
            V.tensor_reduce(sc[:, 0:1], ZB[:, :, :], AX.XY, ALU.add,
                            apply_absolute_value=True).then_inc(dve_q, 1)
            dve.wait_ge(pool_sum, 1)
            V.tensor_scalar(sc[:, 2:3], sc[:, 1:2], 1.0 / (C * C), None, ALU.mult).then_inc(dve_s, 1)
            dve.wait_ge(dve_s, 1)
            V.tensor_scalar(sc[:, 3:4], sc[:, 2:3], FFN_EPS, None, ALU.add).then_inc(dve_s, 1)
            dve.wait_ge(dve_s, 2)
            V.reciprocal(sc[:, 4:5], sc[:, 3:4]).then_inc(dve_q, 1)
            dve.wait_ge(dve_q, 2)
            V.tensor_scalar(ZB[:, :, :], ZB[:, :, :], sc[:, 4:5], ROUND, ALU.mult, ALU.add).then_inc(dve_q, 1)
            dve.wait_ge(act_c, 2)

            def clamp_k(b, c):
                dve.wait_ge(act_k, CREDIT + 8 * b + c + 1)
                V.tensor_scalar(KV[:, c % 2, 0, :], KV[:, c % 2, 0, :], math.exp(K_CLAMP), None,
                                ALU.min).then_inc(dve_min, 1)

            def recurrence(b, c):
                t, j = divmod(c, CH)
                kv = KV[:, c % 2]
                dve.wait_ge(pe_g, CREDIT + 24 * b + 3 * c + 2)
                dve.wait_ge(dve_min, 8 * b + c + 1)
                V.tensor_tensor(kv[:, 1, :], kv[:, 0, :], KVR[:, 1, :], ALU.mult).then_inc(dve_kv, 1)
                dve.wait_ge(dve_sum, CREDIT + 8 * b + c)
                if t == 0:
                    V.memset(S[:, :, 0:1], 0.0)
                else:
                    V.tensor_copy(S[:, :, 0:1], state[:, j, :].rearrange("p (a o) -> p a o", o=1))
                dec = decay[:, j:j + 1].to_broadcast([P, TILE])
                for i in range(2):
                    if i == 1:
                        dve.wait_ge(dve_kv, CREDIT + 8 * b + c + 1)
                    last = V.tensor_tensor_scan(S[:, i, 1:TILE + 1], dec, kv[:, i, :],
                                                0.0 if t == 0 else state[:, j, i:i + 1], ALU.mult, ALU.add)
                last.then_inc(dve_scan, 1)
                dve.wait_ge(dve_scan, 8 * b + c + 1)
                if t == 0:
                    V.tensor_copy(state[:, j, :].rearrange("p (a o) -> p a o", o=1), S[:, :, TILE:TILE + 1])
                V.scalar_tensor_tensor(kv, kv, first[:, j:j + 1], S[:, :, 0:TILE], ALU.mult,
                                       ALU.add).then_inc(dve_sum, 1)

            def denominator(b, c):
                dve.wait_ge(act_ls, 8 * b + c + 1)
                V.tensor_tensor(E[:, c % 2, :], E[:, c % 2, :], KV[:, c % 2, 0, :], ALU.add).then_inc(dve_l, 1)

            def rwkv(b, c):
                dve.wait_ge(act_y, 8 * b + c + 1)
                V.tensor_tensor(KV[:, c % 2, 1, :], KV[:, c % 2, 1, :], E[:, c % 2, :], ALU.mult).then_inc(dve_rw, 1)

            def rwkv_lo(b, c):
                dve.wait_ge(act_rh, 8 * b + c + 1)
                V.tensor_tensor(RL[:, c % CH, :], KV[:, c % 2, 1, :], RH[:, c % CH, :].bitcast(F32),
                                ALU.subtract).then_inc(dve_rl, 1)

            def add_out(b, ph, what):
                use = bank_use(b, ph, what)
                t = int(what[-1])
                if what.startswith("attn") or what.startswith("own"):
                    tile = X[t]
                    dve.wait_ge(pool_xn, normed_count(b, f"ffn_own{t}"))
                else:
                    tile = ZB
                    dve.wait_ge(s_park, 32 * (b - HALF) + 16 * t + 16)
                if ph == "B" and what.startswith("attn"):
                    dve.wait_ge(dve_out, BANKS + bank_use(b, ph, f"own{t}") + Q)
                for q in range(Q):
                    dve.wait_ge(pe_out, use + q + 1)
                    if what.startswith("attn"):
                        V.tensor_tensor(tile[:, q, :], tile[:, q, :], OUT[:, q, :], ALU.add).then_inc(dve_out, 1)
                    else:
                        V.scalar_tensor_tensor(tile[:, q, :], OUT[:, q, :], sc[:, 7:8], tile[:, q, :],
                                               ALU.mult, ALU.add).then_inc(dve_out, 1)

            ADD_AFTER = {6: "own0", 10: "other0", 18: "own1", 22: "other1"}

            STATS_AT = {0: ["other0"], 4: ["own1"], 12: ["other1"], 16: ["next0"]}

            def tile_stats(b, tile, is_last):
                if tile == "next0":
                    if is_last:
                        return
                    dve.wait_ge(s_x[0], 16 * b + 32)
                    src = X[0]
                elif tile == "own1":
                    dve.wait_ge(s_x[1], 16 * b + 16)
                    src = X[1]
                else:
                    dve.wait_ge(s_oth, 32 * b + 16 * (int(tile[-1]) + 1))
                    src = ZA
                stats_of(stats_number(b, tile), src, (STATS_ORDER.index(tile) + 1) % 2)

            def batch(b, ph, is_last=False):
                last = None
                for g in range(GROUPS):
                    c, m = divmod(g, 3)
                    n = slot_ahead(g, is_last)
                    if last is not None:
                        low_part(b, ph, last)
                    if n is not None:
                        mix_or_clip(b, ph, n)
                    last = n
                    for what in STATS_AT.get(g, ()):
                        tile_stats(b, what, is_last)
                    if m == 0:
                        clamp_k(b, c)
                        if c:
                            denominator(b, c - 1)
                            if c == CH:
                                rwkv(b, c - 1)
                                rwkv_lo(b, c - 1)
                                add_out(b, ph, "attn0")
                    elif m == 1:
                        if c and c != CH:
                            rwkv(b, c - 1)
                        recurrence(b, c)
                    elif m == 2 and c and c != CH:
                        rwkv_lo(b, c - 1)
                    if ph == "B" and g in ADD_AFTER:
                        add_out(b, ph, ADD_AFTER[g])
                if last is not None:
                    low_part(b, ph, last)
                denominator(b, 2 * CH - 1)
                rwkv(b, 2 * CH - 1)
                rwkv_lo(b, 2 * CH - 1)
                add_out(b, ph, "attn1")
                if ph == "A":
                    dve.wait_ge(dve_lo, RING + slots_before(b, ph, first_slot("mix_next0")))
                    V.tensor_tensor(mx[:, :], mx[:, :], am[:, :], ALU.max).then_inc(dve_mx, 1)

            with dve.Fori(0, HALF) as b:
                batch(b, "A")
            dve.wait_ge(dve_mx, HALF + 1)
            V.tensor_reduce(sc[:, 5:6], mx[:, :], AX.X, ALU.max).then_inc(dve_s, 1)
            dve.wait_ge(pool_max, 1)
            V.reciprocal(sc[:, 3:4], sc[:, 6:7]).then_inc(dve_s, 1)
            V.scalar_tensor_tensor(sc[:, 7:8], sc[:, 6:7], 1.0 / QB, sc[:, 2:3], ALU.mult, ALU.mult)
            dve.wait_ge(dve_s, 4)
            V.tensor_scalar(gamq[:, :], gam[:, :], QB, sc[:, 3:4], ALU.mult, ALU.mult)
            V.tensor_scalar(betq[:, :], bet[:, :], QB, sc[:, 3:4], ALU.mult, ALU.mult).then_inc(dve_s, 1)
            dve.wait_ge(dve_s, 5)
            with dve.Fori(HALF, B - 1) as b:
                batch(b, "B")
            batch(B - 1, "B", is_last=True)

        @block.gpsimd
        def _(pool):
            G = nc.gpsimd
            pool.sem_inc(pool_step, STEPS)
            G.memset(ident[:, :], 0.0).then_inc(pool_id, 1)
            pool.wait_ge(pool_id, 1)
            G.affine_select(out=ident[:, :], in_=ident[:, :], compare_op=ALU.not_equal, fill=1.0, base=0,
                            pattern=[[-1, P]], channel_multiplier=1).then_inc(pool_id, 1)

            def scales(i, r, dst):
                mean, var = mv[:, r, :, 0], mv[:, r, :, 1]
                k = [0]

                def step(instruction):
                    k[0] += 1
                    instruction.then_inc(pool_step, 1)
                    pool.wait_ge(pool_step, STEPS + i * STEPS + k[0])
                    pool.sem_inc(pool_past, 1)

                pool.wait_ge(dve_mv, i + 1)
                pool.sem_inc(pool_past, 1)
                step(G.tensor_scalar(st[:, 0, :], var, 1.0, LN_EPS, ALU.mult, ALU.add))
                step(G.tensor_tensor(dst[:, 0, :], st[:, 0, :], half_neg[:, :], ALU.pow))
                step(G.tensor_tensor(st[:, 1, :], var, dst[:, 0, :], ALU.mult))
                step(G.tensor_tensor(st[:, 2, :], st[:, 1, :], dst[:, 0, :], ALU.mult))
                step(G.tensor_scalar(st[:, 3, :], st[:, 2, :], 1.0, FFN_LN_EPS, ALU.mult, ALU.add))
                step(G.tensor_tensor(st[:, 4, :], st[:, 3, :], half_neg[:, :], ALU.pow))
                G.tensor_scalar(st[:, 5, :], mean, -1.0, 0.0, ALU.mult, ALU.add)
                step(G.tensor_tensor(dst[:, 2, :], st[:, 4, :], dst[:, 0, :], ALU.mult))
                G.tensor_tensor(dst[:, 1, :], st[:, 5, :], dst[:, 0, :], ALU.mult)
                step(G.tensor_tensor(dst[:, 3, :], st[:, 5, :], dst[:, 2, :], ALU.mult))
                assert k[0] == STEPS
                return k

            def normalise(dst, src, stats, kind, done):
                pool.sem_inc(pool_past, 1)
                for q in range(Q):
                    last = G.tensor_scalar(dst[:, q, :], src[:, q, :], stats[:, 2 * kind, q:q + 1],
                                           stats[:, 2 * kind + 1, q:q + 1], ALU.mult, ALU.add)
                last.then_inc(done, 1)

            pool.wait_ge(dve_c, 1)
            scales(0, 0, own[:, 0])
            normalise(XN, X[0], own[:, 0], 0, pool_xn)
            pool.wait_ge(dve_q, 1)
            G.partition_all_reduce(sc[:, 1:2], sc[:, 0:1], P, bass.bass_isa.ReduceOp.add).then_inc(pool_sum, 1)

            def scales_of(b, tile, dst):
                scales(stats_number(b, tile), (STATS_ORDER.index(tile) + 1) % 2, dst)

            def batch(b, is_last=False):
                pool.wait_ge(pe_t, slots_before(b, "any", 0))
                normalise(XN, X[0], own[:, 0], 1, pool_xn)
                scales_of(b, "other0", oth)
                normalise(ZA, ZA, oth, 1, pool_za)
                scales_of(b, "own1", own[:, 1])
                pool.wait_ge(pe_t, slots_before(b, "any", first_slot("ffn_own0") + CH))
                normalise(XN, X[1], own[:, 1], 0, pool_xn)
                pool.wait_ge(pe_t, slots_before(b, "any", first_slot("mix_own1") + CH))
                normalise(XN, X[1], own[:, 1], 1, pool_xn)
                scales_of(b, "other1", oth)
                normalise(ZA, ZA, oth, 1, pool_za)
                if not is_last:
                    scales_of(b, "next0", own[:, 0])
                    pool.wait_ge(pe_t, slots_before(b, "any", first_slot("ffn_own1") + CH))
                    normalise(XN, X[0], own[:, 0], 0, pool_xn)

            with pool.Fori(0, HALF) as b:
                batch(b)
            pool.wait_ge(dve_s, 3)
            G.partition_all_reduce(sc[:, 6:7], sc[:, 5:6], P, bass.bass_isa.ReduceOp.max).then_inc(pool_max, 1)
            with pool.Fori(HALF, B - 1) as b:
                batch(b)
            batch(B - 1, is_last=True)


_INS = ["L0_attn_x", "L0_attn_time_decay", "L0_attn_time_first", "L0_attn_time_mix", "L0_attn_Wk",
        "L0_attn_Wv", "L0_attn_Wr", "L0_attn_Wo", "L0_ffn_weight", "L0_ffn_ln_gamma", "L0_ffn_ln_beta"]


def kernel(**inputs):
    import numpy as np
    import concourse.bacc as bacc
    from concourse.bass_utils import run_bass_kernel_spmd

    nc = bacc.Bacc("TRN2", target_bir_lowering=False, num_devices=1)
    arrays, args = {}, []
    for name in _INS:
        a = np.ascontiguousarray(inputs[name])
        arrays[f"in_{name}"] = a
        args.append(nc.dram_tensor(f"in_{name}", a.shape, mybir.dt.from_np(a.dtype), kind="ExternalInput").ap())
    shape = arrays["in_L0_attn_x"].shape
    result = nc.dram_tensor("out", shape, F32, kind="ExternalOutput").ap()
    mixed_decay_kernel(nc, *args, result)
    r = run_bass_kernel_spmd(nc, [arrays], core_ids=[0])
    return r.results[0]["out"]
```

```python
from contextlib import ExitStack
import math

import concourse.bass as bass
from concourse import mybir

F32 = mybir.dt.float32
F32R = mybir.dt.float32r
ALU = mybir.AluOpType
ACT = mybir.ActivationFunctionType
AX = mybir.AxisListType

P = 128
TILE = 512
LN_EPS = 1e-5
FFN_LN_EPS = 1e-3
FFN_EPS = 1e-5
QB = 128.0
K_CLAMP = 60.0
K_EPS = 1e-16
POOL_CHUNKS, ACT_CHUNKS = (0, 1), (2, 3)
ROUND = 1.5 * 2.0 ** 23

SLOT_KINDS = ["ffn_own0", "ffn_other0", "mix_own1", "ffn_own1", "ffn_other1", "mix_next0"]
SLOTS = [(kind, ch) for kind in SLOT_KINDS for ch in range(4)]
STATS_ORDER = ["other0", "own1", "other1", "next0"]
FFN_AFTER = {4: "own0", 8: "other0", 16: "own1", 20: "other1"}
BANK_USES = {"A": ["attn0", "attn1"],
             "B": ["own0", "other0", "attn0", "own1", "other1", "attn1"]}
ATTN0_AFTER = 12


def mixed_decay_kernel(nc, x, time_decay, time_first, time_mix, Wk, Wv, Wr, Wo, Wf, ln_gamma, ln_beta, out):
    B, T, C = x.shape
    H = time_decay.shape[0]
    CH = C // P
    Q = TILE // P
    D = C // H
    HPC = P // D
    HALF = B // 2
    assert (CH, Q, T // TILE, 2 * HALF) == (4, 4, 2, B)
    CHUNKS = 2 * CH
    GROUPS = 3 * CHUNKS

    x_t = x.rearrange("b (t q p) c -> b t p q c", q=Q, p=P)
    out_t = out.rearrange("b (t q p) c -> b t p q c", q=Q, p=P)
    scratch = nc.dram_tensor("attn_scratch", (HALF, T, C), F32, kind="Internal").ap()
    scratch_t = scratch.rearrange("b (t q p) c -> b t p q c", q=Q, p=P)

    with ExitStack() as ctx:
        def sb(name, shape, dt=F32):
            return ctx.enter_context(nc.sbuf_tensor(name, shape, dt))

        def sem(name):
            return ctx.enter_context(nc.semaphore(name))

        names = ["k", "v", "r", "o"]
        WH = {n: sb(f"w{n}_hi", [P, CH, C], F32R) for n in names}
        WL = {n: sb(f"w{n}_lo", [P, CH, C], F32R) for n in names}
        WQ = sb("w_ternary", [P, CH, C], F32R)
        X = [sb(f"x{t}", [P, Q, C]) for t in range(2)]
        XN = sb("normed", [P, Q, C])
        ZA = sb("other", [P, Q, C])
        ZB = sb("parked", [P, Q, C])
        U = sb("evacuated", [P, 2, TILE])
        WS = sb("shifted_part", [P, 2, TILE])
        XH = [sb(f"xm_hi{t}", [P, CH, TILE], F32R) for t in range(2)]
        XL = [sb(f"xm_lo{t}", [P, CH, TILE], F32R) for t in range(2)]
        AH = sb("ffn_hi", [P, CH, TILE], F32R)
        AL = sb("ffn_lo", [P, CH, TILE], F32R)
        KV = sb("k_and_kv", [P, 2, 2, TILE])
        E = sb("gate", [P, 2, TILE])
        S = sb("scans", [P, 2, TILE + 1])
        RH = sb("rwkv_hi", [P, CH, TILE], F32R)
        RL = sb("rwkv_lo", [P, CH, TILE], F32R)
        ident = sb("ident", [P, P])
        tmx = sb("time_mix", [P, CH])
        tmx1 = sb("one_minus_mix", [P, CH])
        decay = sb("decay", [P, CH])
        first = sb("first", [P, CH])
        gam = sb("gamma_in", [P, CH])
        bet = sb("beta_in", [P, CH])
        gamq = sb("gamma_scaled", [P, CH])
        betq = sb("beta_scaled", [P, CH])
        state = sb("state", [P, CH, 2])
        last_x = sb("last_token", [P, CH])
        bnst = sb("bn_stats", [P, Q, 6])
        mv = sb("mean_var", [P, 2, Q, 2])
        half_neg = sb("minus_half", [P, Q])
        st = sb("stat_work", [P, 6, Q])
        own = sb("own_stats", [P, 2, 4, Q])
        oth = sb("other_stats", [P, 4, Q])
        am = sb("absmax", [P, 4 * CH])
        mx = sb("absmax_all", [P, 4 * CH])
        rows = sb("rows", [3 * CH, P])
        heads = sb("heads", [2 * CH, HPC])
        head_rows = sb("head_rows", [2 * CH, P])
        sc = sb("scalars", [P, 8])
        eps_k = sb("k_eps", [P, 1])
        round_c = sb("minus_round", [P, 1])
        one_c = sb("one", [P, 1])

        KVR = ctx.enter_context(nc.psum_tensor("kvr", [P, 3, TILE], F32))
        OUT = ctx.enter_context(nc.psum_tensor("out_banks", [P, Q, C], F32))
        TB = ctx.enter_context(nc.psum_tensor("transposed", [P, TILE], F32))

        s_x = [sem(f"x_loaded{t}") for t in range(2)]
        s_xst = [sem(f"x_stored{t}") for t in range(2)]
        s_oth = sem("other_loaded")
        s_park = sem("parked_loaded")
        s_parkst = sem("parked_stored")
        s_w = [sem(f"w_loaded_{n}") for n in names + ["f"]]
        s_small = sem("small_loaded")
        pe_w = sem("pe_weights_transposed")
        pe_g = sem("pe_groups")
        pe_t = sem("pe_slots")
        pe_out = sem("pe_out_banks")
        pe_rw = sem("pe_rwkv_chunks_read")
        pe_ah = sem("pe_ffn_chunks_read")
        pe_c = sem("pe_constants_transposed")
        act_w = sem("act_w_hi")
        act_k = sem("act_exp_k")
        act_r = sem("act_exp_r")
        act_xn = sem("act_normed")
        act_za = sem("act_other_normed")
        act_q = sem("act_ternary")
        act_le = sem("act_ln_gate")
        act_ls = sem("act_ln_sums")
        act_y = sem("act_quotient")
        act_rh = sem("act_rwkv_hi")
        act_u = sem("act_evacuated")
        act_h = sem("act_hi")
        act_c = sem("act_constants")
        dve_c = sem("dve_constants")
        dve_w = sem("dve_w_lo")
        dve_q = sem("dve_quantise")
        dve_min = sem("dve_k_clamped")
        dve_kv = sem("dve_kv")
        dve_scan = sem("dve_scans")
        dve_sum = sem("dve_sums")
        dve_l = sem("dve_log_denominator")
        dve_rw = sem("dve_rwkv")
        dve_rl = sem("dve_rwkv_lo")
        dve_x = sem("dve_mixed_or_clipped")
        dve_lo = sem("dve_lo")
        dve_mx = sem("dve_absmax_all")
        dve_bn = sem("dve_bn_stats")
        dve_mv = sem("dve_mean_var")
        dve_out = sem("dve_out_banks_added")
        dve_s = sem("dve_scalars")
        pool_id = sem("pool_ident")
        pool_step = sem("pool_steps")
        dve_past = sem("dve_past_wait")
        pool_past = sem("pool_past_wait")
        pool_xn = sem("pool_normed")
        pool_za = sem("pool_other_normed")
        pool_sum = sem("pool_weight_sum")
        pool_max = sem("pool_gamma")

        STEPS, MIX_STEPS = 9, 3
        CREDIT = 1
        RING = 2
        BANKS = 4

        def slots_before(b, ph, n):
            return n if ph == "P" else CH + len(SLOTS) * b + n

        def splits_before(b, ph, n):
            if ph == "P":
                return n
            if ph == "A":
                return CH + 2 * CH * b + sum(kind.startswith("mix") for kind, _ in SLOTS[:n])
            return CH + 2 * CH * HALF + len(SLOTS) * (b - HALF) + n

        def is_split(ph, n):
            return ph != "A" or SLOTS[n][0].startswith("mix")

        def slot_of(ph, n):
            return ("mix_next0", n) if ph == "P" else SLOTS[n]

        def first_slot(kind):
            return SLOTS.index((kind, 0))

        def normed_count(b, kind):
            return 4 * b + [k for k in SLOT_KINDS if "other" not in k].index(kind) + 1

        def stats_number(b, tile):
            return 4 * b + STATS_ORDER.index(tile) + 1

        def bank_use(b, ph, what):
            before = Q * BANK_USES[ph].index(what)
            if ph == "A":
                return 2 * Q * b + before
            return 2 * Q * HALF + 6 * Q * (b - HALF) + before

        def slot_ahead(g, is_last):
            return None if is_last and SLOTS[g][0] == "mix_next0" else g

        def ahead_of_part2(n):
            return n is not None and (n + 1 == len(SLOTS) or "mix" in SLOTS[n][0] or "mix" in SLOTS[n + 1][0])

        weight_banks = [OUT[:, i, :] for i in range(Q)]
        first_banks = [TB[:, :]] + [KVR[:, i, :] for i in range(3)]
        PROLOGUE = ["k", "v", "r", "slots", "o"]

        RAW = {"k": ZB, "v": ZA, "r": X[1], "o": KV[:, :, :, :].rearrange("p a b n -> p (a b) n")}

        block = ctx.enter_context(nc.Block())

        @block.sync
        def _(sp):
            for i, src in enumerate((time_mix.rearrange("a b (j p) -> (a b j) p", p=P),
                                     ln_gamma.rearrange("(j p) -> j p", p=P),
                                     ln_beta.rearrange("(j p) -> j p", p=P))):
                sp.dma_start(rows[i * CH:(i + 1) * CH, :], src).then_inc(s_small, 16)
            for i, src in enumerate((time_decay, time_first)):
                sp.dma_start(heads[i * CH:(i + 1) * CH, :],
                              src.rearrange("(j g) o -> j (g o)", g=HPC)).then_inc(s_small, 16)
            sp.dma_start(X[0][:, :, :], x_t[0, 0]).then_inc(s_x[0], 16)
            for i, (n, w) in enumerate(zip(names, (Wk, Wv, Wr, Wo))):
                raw = RAW[n]
                sp.dma_start(raw if n == "o" else raw[:, :, :],
                             w.rearrange("(i p) c -> p i c", p=P)).then_inc(s_w[i], 16)
            sp.wait_ge(pe_w, CH)
            sp.dma_start(ZB[:, :, :], Wf.rearrange("(i p) c -> p i c", p=P)).then_inc(s_w[4], 16)
            sp.wait_ge(pe_w, 2 * CH)
            sp.dma_start(ZA[:, :, :], x_t[HALF, 0]).then_inc(s_oth, 16)
            sp.wait_ge(pe_w, 3 * CH)
            sp.dma_start(X[1][:, :, :], x_t[0, 1]).then_inc(s_x[1], 16)

            def batch(b, ph, is_last=False):
                own_dst, own_b = (scratch_t, b) if ph == "A" else (out_t, b)
                sp.wait_ge(pe_t, slots_before(b, ph, first_slot("ffn_other0") + CH))
                sp.dma_start(ZA[:, :, :], x_t[(b + HALF) % B, 1]).then_inc(s_oth, 16)
                if ph == "B":
                    sp.wait_ge(dve_out, BANKS + bank_use(b, ph, "other0") + Q)
                    sp.dma_start(out_t[b - HALF, 0], ZB[:, :, :]).then_inc(s_parkst, 16)
                    sp.wait_ge(s_parkst, 32 * (b - HALF) + 16)
                    sp.dma_start(ZB[:, :, :], scratch_t[b - HALF, 1]).then_inc(s_park, 16)
                sp.wait_ge(dve_out, BANKS + bank_use(b, ph, "attn0") + Q)
                sp.dma_start(own_dst[own_b, 0], X[0][:, :, :]).then_inc(s_xst[0], 16)
                sp.wait_ge(s_xst[0], 16 * b + 16)
                if not is_last:
                    sp.dma_start(X[0][:, :, :], x_t[b + 1, 0]).then_inc(s_x[0], 16)
                    sp.wait_ge(pe_t, slots_before(b, ph, first_slot("ffn_other1") + CH))
                    sp.dma_start(ZA[:, :, :], x_t[(b + HALF + 1) % B, 0]).then_inc(s_oth, 16)
                if ph == "B":
                    sp.wait_ge(dve_out, BANKS + bank_use(b, ph, "other1") + Q)
                    sp.dma_start(out_t[b - HALF, 1], ZB[:, :, :]).then_inc(s_parkst, 16)
                if is_last:
                    for q in range(Q):
                        sp.wait_ge(dve_out, BANKS + bank_use(b, ph, "attn1") + q + 1)
                        sp.dma_start(out_t[b, 1][:, q, :], X[1][:, q, :]).then_inc(s_xst[1], 16)
                else:
                    sp.wait_ge(dve_out, BANKS + bank_use(b, ph, "attn1") + Q)
                    sp.dma_start(own_dst[own_b, 1], X[1][:, :, :]).then_inc(s_xst[1], 16)
                if ph == "B":
                    sp.wait_ge(s_parkst, 32 * (b - HALF) + 32)
                    if not is_last:
                        sp.dma_start(ZB[:, :, :], scratch_t[b - HALF + 1, 0]).then_inc(s_park, 16)
                sp.wait_ge(s_xst[1], 16 * b + (16 * Q if is_last else 16))
                if not is_last:
                    sp.dma_start(X[1][:, :, :], x_t[b + 1, 1]).then_inc(s_x[1], 16)

            with sp.Fori(0, HALF) as b:
                batch(b, "A")
            sp.wait_ge(act_q, 1)
            sp.dma_start(ZB[:, :, :], scratch_t[0, 0]).then_inc(s_park, 16)
            with sp.Fori(HALF, B - 1) as b:
                batch(b, "B")
            batch(B - 1, "B", is_last=True)

        @block.tensor
        def _(pe):
            pe.sem_inc(pe_g, CREDIT)
            pe.sem_inc(pe_rw, BANKS - 1)
            pe.sem_inc(pe_ah, BANKS - 1)

            def transpose_slot(b, ph, n, src):
                _, ch = slot_of(ph, n)
                bank = first_banks[n] if ph == "P" else TB[:, :]
                for q in range(Q):
                    last = nc.tensor.transpose(bank[:, q * P:(q + 1) * P], src[:, q, ch * P:(ch + 1) * P],
                                               ident[:, :])
                last.then_inc(pe_t, 1)

            pe.wait_ge(pool_id, 2)
            pe.wait_ge(s_small, 16 * 5)
            nc.tensor.transpose(TB[:, 0:3 * CH], rows[:, :], ident[0:3 * CH, 0:3 * CH]).then_inc(pe_c, 1)
            pe.wait_ge(dve_c, 2)
            nc.tensor.transpose(TB[:, 3 * CH:5 * CH], head_rows[:, :], ident[0:2 * CH, 0:2 * CH]).then_inc(pe_c, 1)
            unit = 0
            for n in PROLOGUE:
                if n == "slots":
                    pe.wait_ge(pool_xn, 1)
                    pe.wait_ge(dve_c, 3)
                    for m in range(CH):
                        transpose_slot(0, "P", m, XN)
                    continue
                pe.wait_ge(s_w[names.index(n)], 16)
                for ch in range(CH):
                    if unit >= len(weight_banks):
                        pe.wait_ge(dve_w, unit - len(weight_banks) + 1)
                    bank = weight_banks[unit % len(weight_banks)]
                    for j in range(C // P):
                        last = nc.tensor.transpose(bank[:, j * P:(j + 1) * P],
                                                   RAW[n][:, j, ch * P:(ch + 1) * P], ident[:, :])
                    last.then_inc(pe_w, 1)
                    unit += 1
            pe.wait_ge(dve_w, CH)
            pe.wait_ge(act_u, CH)

            def slot(b, ph, n):
                kind, _ = slot_of(ph, n)
                pe.wait_ge(act_u, slots_before(b, ph, n))
                if n % CH == 0:
                    if "other" in kind:
                        for normed in (pool_za, act_za):
                            pe.wait_ge(normed, 2 * b + int(kind[-1]) + 1)
                    else:
                        for normed in (pool_xn, act_xn):
                            pe.wait_ge(normed, CREDIT + normed_count(b, kind))
                transpose_slot(b, ph, n, ZA if "other" in kind else XN)

            def project(b, ph, g):
                c, m = divmod(g, 3)
                t, j = divmod(c, CH)
                w = names[m]
                if m:
                    pe.wait_ge(dve_w, (m + 1) * CH)
                pe.wait_ge((act_k, dve_kv, act_r)[m], CREDIT + CHUNKS * b + c)
                for ch in range(CH):
                    if j == 0 and m == 0:
                        slot0 = first_slot("mix_own1") if t == 1 else -CH
                        pe.wait_ge(dve_lo, RING + slots_before(b, ph, slot0 + ch) + 1)
                    hi = WH[w][:, ch, j * P:(j + 1) * P]
                    lo = WL[w][:, ch, j * P:(j + 1) * P]
                    nc.tensor.matmul(KVR[:, m, :], hi, XH[t][:, ch, :], start=(ch == 0), stop=False)
                    nc.tensor.matmul(KVR[:, m, :], hi, XL[t][:, ch, :], start=False, stop=False)
                    last = nc.tensor.matmul(KVR[:, m, :], lo, XH[t][:, ch, :], start=False, stop=(ch == CH - 1))
                last.then_inc(pe_g, 1)

            def attn_out(b, ph, t):
                first_bank = bank_use(b, ph, f"attn{t}")
                pe.wait_ge(dve_w, 4 * CH)
                for j in range(CH):
                    pe.wait_ge(dve_rl, RING + CHUNKS * b + 4 * t + j + 1)
                    for q in range(Q):
                        if j == 0:
                            pe.wait_ge(dve_out, first_bank + q + 1)
                        hi, lo = (r[:, j, q * P:(q + 1) * P] for r in (RH, RL))
                        nc.tensor.matmul(OUT[:, q, :], hi, WH["o"][:, j, :], start=(j == 0), stop=False)
                        nc.tensor.matmul(OUT[:, q, :], hi, WL["o"][:, j, :], start=False, stop=False)
                        last = nc.tensor.matmul(OUT[:, q, :], lo, WH["o"][:, j, :], start=False,
                                                stop=(j == CH - 1))
                        if j == CH - 1:
                            last.then_inc(pe_out, 1)
                    if j < CH - 1:
                        last.then_inc(pe_rw, 1)

            def ffn_out(b, what):
                first_bank = bank_use(b, "B", what)
                start_slot = first_slot(f"ffn_{what}")
                for ch in range(CH):
                    pe.wait_ge(dve_lo, RING + slots_before(b, "any", start_slot + ch) + 1)
                    for q in range(Q):
                        if ch == 0:
                            pe.wait_ge(dve_out, first_bank + q + 1)
                        nc.tensor.matmul(OUT[:, q, :], AH[:, ch, q * P:(q + 1) * P], WQ[:, ch, :],
                                         start=(ch == 0), stop=False)
                        last = nc.tensor.matmul(OUT[:, q, :], AL[:, ch, q * P:(q + 1) * P], WQ[:, ch, :],
                                                start=False, stop=(ch == CH - 1))
                        if ch == CH - 1:
                            last.then_inc(pe_out, 1)
                    if ch < CH - 1:
                        last.then_inc(pe_ah, 1)

            def batch(b, ph, is_last=False):
                for g in range(GROUPS):
                    n = slot_ahead(g, is_last)
                    if g == ATTN0_AFTER:
                        project(b, ph, g)
                        slot(b, ph, n)
                    else:
                        if n is not None:
                            slot(b, ph, n)
                        project(b, ph, g)
                    if ph == "B" and g in FFN_AFTER:
                        ffn_out(b, FFN_AFTER[g])
                    if g == ATTN0_AFTER:
                        attn_out(b, ph, 0)
                attn_out(b, ph, 1)

            with pe.Fori(0, HALF) as b:
                batch(b, "A")
            pe.wait_ge(act_q, 1)
            with pe.Fori(HALF, B - 1) as b:
                batch(b, "B")
            batch(B - 1, "B", is_last=True)

        @block.scalar
        def _(act):
            nc.scalar.preload_act_table_set("natural_log_exp_and_others")
            act.sem_inc(act_k, CREDIT)
            act.sem_inc(act_r, CREDIT)
            act.sem_inc(act_xn, 2 * CREDIT)

            def evacuate(b, ph, n):
                kind, ch = slot_of(ph, n)
                bank = first_banks[n] if ph == "P" else TB[:, :]
                m = slots_before(b, ph, n)
                act.wait_ge(pe_t, m + 1)
                act.wait_ge(dve_lo, m + 1)
                r = n % 2
                if kind.startswith("mix"):
                    nc.scalar.activation(U[:, r, :], bank, ACT.Copy, scale=tmx[:, ch:ch + 1])
                    nc.scalar.activation(WS[:, r, :], bank, ACT.Copy,
                                         scale=tmx1[:, ch:ch + 1]).then_inc(act_u, 1)
                elif ph == "A":
                    nc.scalar.activation(U[:, r, :], bank, ACT.Identity, bias=bet[:, ch:ch + 1],
                                         scale=gam[:, ch:ch + 1]).then_inc(act_u, 1)
                else:
                    nc.scalar.activation(U[:, r, :], bank, ACT.Identity, bias=betq[:, ch:ch + 1],
                                         scale=gamq[:, ch:ch + 1]).then_inc(act_u, 1)

            def high_part(b, ph, n):
                kind, ch = slot_of(ph, n)
                if not is_split(ph, n):
                    return
                act.wait_ge(dve_x, splits_before(b, ph, n) + 1)
                if kind.startswith("mix"):
                    t = int(kind[-1])
                    if kind == "mix_own1":
                        act.wait_ge(pe_g, CREDIT + GROUPS * b)
                    elif ph != "P":
                        act.wait_ge(pe_g, CREDIT + GROUPS * b + GROUPS // 2)
                    dst = XH[t][:, ch, :]
                else:
                    f = 4 * (b - HALF) + ["ffn_own0", "ffn_other0", "ffn_own1", "ffn_other1"].index(kind)
                    if ch < CH - 1:
                        act.wait_ge(pe_ah, 3 * f + ch + 1)
                    else:
                        before = {"ffn_own0": "attn1", "ffn_other0": "own0", "ffn_own1": "attn0",
                                  "ffn_other1": "own1"}[kind]
                        if kind == "ffn_own0":
                            act.wait_ge(pe_out, bank_use(b, ph, "own0"))
                        else:
                            act.wait_ge(pe_out, bank_use(b, ph, before) + Q)
                    dst = AH[:, ch, :]
                nc.scalar.activation(dst, U[:, n % 2, :], ACT.Copy).then_inc(act_h, 1)

            def normalise(b, kind):
                t = int(kind[-1])
                if "other" in kind:
                    tile, dst, src, stats = f"other{t}", ZA, ZA, oth
                else:
                    tile, dst, src, stats = ("own1" if t else "next0"), XN, X[t], own[:, t]
                ffn = kind.startswith("ffn")
                i = 4 * b if kind == "ffn_own0" else stats_number(b, tile)
                act.wait_ge(pool_step, STEPS + STEPS * i + (STEPS if ffn else MIX_STEPS))
                for q in ACT_CHUNKS:
                    last = nc.scalar.activation(dst[:, q, :], src[:, q, :], ACT.Identity,
                                                bias=stats[:, 2 * ffn + 1, q:q + 1],
                                                scale=stats[:, 2 * ffn, q:q + 1])
                last.then_inc(act_za if "other" in kind else act_xn, 1)

            NORMALISE_AT = {2: "ffn_other0", 6: "mix_own1", 14: "ffn_other1", 18: "mix_next0"}

            unit = 0
            for n in PROLOGUE:
                if n == "slots":
                    act.wait_ge(dve_c, 4)
                    for pair in range(0, CH, 2):
                        for m in (pair, pair + 1):
                            evacuate(0, "P", m)
                        for m in (pair, pair + 1):
                            high_part(0, "P", m)
                    nc.scalar.activation(decay[:, :], decay[:, :], ACT.Exp, scale=-1.0).then_inc(act_c, 1)
                    continue
                for ch in range(CH):
                    act.wait_ge(pe_w, unit + 1)
                    nc.scalar.activation(WH[n][:, ch, :], weight_banks[unit % len(weight_banks)],
                                         ACT.Copy).then_inc(act_w, 1)
                    unit += 1
                if n == "k":
                    act.wait_ge(dve_c, 3)
                    nc.scalar.activation(first[:, :], first[:, :], ACT.Exp)
                    nc.scalar.activation(decay[:, :], decay[:, :], ACT.Exp).then_inc(act_c, 1)
                    act.wait_ge(act_c, 1)

            def exp_k(b, c):
                act.wait_ge(pe_g, CREDIT + GROUPS * b + 3 * c + 1)
                act.wait_ge(dve_rl, CHUNKS * b + c + 1)
                nc.scalar.activation(KV[:, c % 2, 0, :], KVR[:, 0, :], ACT.Exp).then_inc(act_k, 1)

            def exp_r(b, c):
                act.wait_ge(pe_g, CREDIT + GROUPS * b + 3 * c + 3)
                nc.scalar.activation(E[:, c % 2, :], KVR[:, 2, :], ACT.Exp, scale=-1.0).then_inc(act_r, 1)
                act.wait_ge(act_r, CREDIT + CHUNKS * b + c + 1)
                nc.scalar.activation(E[:, c % 2, :], E[:, c % 2, :], ACT.Ln, bias=one_c[:, :]).then_inc(act_le, 1)

            def ln_sums(b, c):
                act.wait_ge(dve_sum, CREDIT + CHUNKS * b + c + 1)
                nc.scalar.activation(KV[:, c % 2, 0, :], KV[:, c % 2, 0, :], ACT.Ln,
                                     bias=eps_k[:, :]).then_inc(act_ls, 1)

            def quotient(b, c):
                act.wait_ge(dve_l, CHUNKS * b + c + 1)
                nc.scalar.activation(E[:, c % 2, :], E[:, c % 2, :], ACT.Exp, scale=-1.0).then_inc(act_y, 1)

            def rwkv_hi(b, ph, c):
                t, j = divmod(c, CH)
                act.wait_ge(dve_rw, CHUNKS * b + c + 1)
                if j < CH - 1:
                    act.wait_ge(pe_rw, 3 * (2 * b + t) + j + 1)
                elif t == 1:
                    act.wait_ge(pe_out, bank_use(b, ph, "attn0") + Q)
                else:
                    act.wait_ge(pe_rw, 3 * (2 * b) + CH - 1)
                    if ph == "B":
                        act.wait_ge(pe_out, bank_use(b, ph, "own0"))
                nc.scalar.activation(RH[:, j, :], KV[:, c % 2, 1, :], ACT.Copy).then_inc(act_rh, 1)

            def batch(b, ph, is_last=False):
                last = None
                for g in range(GROUPS):
                    c, m = divmod(g, 3)
                    n = slot_ahead(g, is_last)
                    part1_first = ahead_of_part2(n)
                    if part1_first:
                        evacuate(b, ph, n)
                    if last is not None:
                        high_part(b, ph, last)
                    if n is not None and not part1_first:
                        evacuate(b, ph, n)
                    last = n
                    if g in NORMALISE_AT and not (is_last and NORMALISE_AT[g] == "mix_next0"):
                        normalise(b, NORMALISE_AT[g])
                    if m == 0:
                        exp_k(b, c)
                        if c:
                            ln_sums(b, c - 1)
                            if c == CH:
                                quotient(b, c - 1)
                                rwkv_hi(b, ph, c - 1)
                    elif m == 1 and c and c != CH:
                        quotient(b, c - 1)
                    elif m == 2:
                        if c and c != CH:
                            rwkv_hi(b, ph, c - 1)
                        if g == ATTN0_AFTER - 1:
                            high_part(b, ph, last)
                            last = None
                            normalise(b, "ffn_own1")
                        exp_r(b, c)
                ln_sums(b, CHUNKS - 1)
                if last is not None:
                    high_part(b, ph, last)
                quotient(b, CHUNKS - 1)
                rwkv_hi(b, ph, CHUNKS - 1)
                if not is_last:
                    normalise(b + 1, "ffn_own0")

            with act.Fori(0, HALF) as b:
                batch(b, "A")
            act.wait_ge(dve_q, 3)
            nc.scalar.activation(WQ[:, :, :], ZB[:, :, :], ACT.Sign, bias=round_c[:, :]).then_inc(act_q, 1)
            act.wait_ge(dve_s, 5)
            with act.Fori(HALF, B - 1) as b:
                batch(b, "B")
            batch(B - 1, "B", is_last=True)

        @block.vector
        def _(dve):
            V = nc.vector
            dve.sem_inc(dve_kv, CREDIT)
            dve.sem_inc(dve_sum, CREDIT)
            dve.sem_inc(dve_rl, RING)
            dve.sem_inc(dve_lo, RING)
            dve.sem_inc(dve_out, BANKS)
            V.memset(eps_k[:, :], K_EPS)
            V.memset(round_c[:, :], -ROUND)
            V.memset(one_c[:, :], 1.0)
            V.memset(half_neg[:, :], -0.5).then_inc(dve_c, 1)
            V.memset(mx[:, :], 0.0).then_inc(dve_mx, 1)

            def stats_of(i, src, place, first=False):
                if not first:
                    dve.wait_ge(pool_step, STEPS * i)
                    dve.wait_ge(dve_mv, i)
                for q in range(Q):
                    last = V.bn_stats(bnst[:, q, :], src[:, q, :])
                last.then_inc(dve_bn, 1)
                dve.wait_ge(dve_bn, i + 1)
                dve.sem_inc(dve_past, 1)
                for q in range(Q):
                    last = V.bn_aggr(mv[:, place, q, :], bnst[:, q, :])
                last.then_inc(dve_mv, 1)

            dve.wait_ge(s_small, 16 * 5)
            V.tensor_copy(head_rows[:, :].rearrange("j (g d) -> j g d", g=HPC),
                          heads[:, :].rearrange("j (g o) -> j g o", o=1).to_broadcast([2 * CH, HPC, D])
                          ).then_inc(dve_c, 1)
            dve.wait_ge(s_x[0], 16)
            stats_of(0, X[0], 0, first=True)
            dve.wait_ge(pe_c, 2)
            for i, dst in enumerate((tmx, gam, bet, decay, first)):
                last = V.tensor_copy(dst[:, :], TB[:, i * CH:(i + 1) * CH])
            last.then_inc(dve_c, 1)
            dve.wait_ge(dve_c, 3)
            V.tensor_scalar(tmx1[:, :], tmx[:, :], -1.0, 1.0, ALU.mult, ALU.add).then_inc(dve_c, 1)

            def tile_stats(b, tile, is_last):
                if tile == "next0":
                    if is_last:
                        return
                    dve.wait_ge(s_x[0], 16 * b + 32)
                    src = X[0]
                elif tile == "own1":
                    dve.wait_ge(s_x[1], 16 * b + 16)
                    src = X[1]
                else:
                    dve.wait_ge(s_oth, 32 * b + 16 * (int(tile[-1]) + 1))
                    src = ZA
                stats_of(stats_number(b, tile), src, (STATS_ORDER.index(tile) + 1) % 2)

            def mix_or_clip(b, ph, n):
                kind, ch = slot_of(ph, n)
                m = slots_before(b, ph, n)
                r = n % 2
                dve.wait_ge(act_u, m + 1)
                if kind.startswith("mix"):
                    if kind.endswith("0"):
                        V.tensor_copy(last_x[:, ch:ch + 1], WS[:, r, TILE - 1:TILE])
                    else:
                        V.tensor_tensor(U[:, r, 0:1], U[:, r, 0:1], last_x[:, ch:ch + 1], ALU.add)
                    V.tensor_tensor(U[:, r, 1:TILE], U[:, r, 1:TILE], WS[:, r, 0:TILE - 1],
                                    ALU.add).then_inc(dve_x, 1)
                elif ph == "A":
                    if n == 0:
                        dve.wait_ge(dve_mx, b + 1)
                    col = n if n < first_slot("mix_own1") else n - CH
                    V.tensor_reduce(am[:, col:col + 1], U[:, r, :], AX.X, ALU.max,
                                    apply_absolute_value=True).then_inc(dve_lo, 1)
                else:
                    V.tensor_scalar(U[:, r, :], U[:, r, :], QB - FFN_EPS, -QB + FFN_EPS, ALU.min,
                                    ALU.max).then_inc(dve_x, 1)

            def low_part(b, ph, n):
                kind, ch = slot_of(ph, n)
                if not is_split(ph, n):
                    return
                dve.wait_ge(act_h, splits_before(b, ph, n) + 1)
                if kind.startswith("mix"):
                    t = int(kind[-1])
                    hi, lo = XH[t][:, ch, :], XL[t][:, ch, :]
                else:
                    hi, lo = AH[:, ch, :], AL[:, ch, :]
                V.tensor_tensor(lo, U[:, n % 2, :], hi.bitcast(F32), ALU.subtract).then_inc(dve_lo, 1)

            unit = 0
            for n in PROLOGUE:
                if n == "slots":
                    for pair in range(0, CH, 2):
                        for m in (pair, pair + 1):
                            mix_or_clip(0, "P", m)
                        for m in (pair, pair + 1):
                            low_part(0, "P", m)
                    dve.wait_ge(s_w[4], 16)
                    V.tensor_reduce(sc[:, 0:1], ZB[:, :, :], AX.XY, ALU.add,
                                    apply_absolute_value=True).then_inc(dve_q, 1)
                    tile_stats(0, "other0", False)
                    dve.wait_ge(pool_sum, 1)
                    V.tensor_scalar(sc[:, 2:3], sc[:, 1:2], 1.0 / (C * C), None, ALU.mult).then_inc(dve_s, 1)
                    dve.wait_ge(dve_s, 1)
                    V.tensor_scalar(sc[:, 3:4], sc[:, 2:3], FFN_EPS, None, ALU.add).then_inc(dve_s, 1)
                    dve.wait_ge(dve_s, 2)
                    V.reciprocal(sc[:, 4:5], sc[:, 3:4]).then_inc(dve_q, 1)
                    dve.wait_ge(dve_q, 2)
                    V.tensor_scalar(ZB[:, :, :], ZB[:, :, :], sc[:, 4:5], ROUND, ALU.mult, ALU.add).then_inc(dve_q, 1)
                    continue
                for ch in range(CH):
                    dve.wait_ge(act_w, unit + 1)
                    V.tensor_tensor(WL[n][:, ch, :], weight_banks[unit % len(weight_banks)],
                                    WH[n][:, ch, :].bitcast(F32), ALU.subtract).then_inc(dve_w, 1)
                    unit += 1

            dve.wait_ge(act_c, 2)

            def clamp_k(b, c):
                dve.wait_ge(act_k, CREDIT + CHUNKS * b + c + 1)
                V.tensor_scalar(KV[:, c % 2, 0, :], KV[:, c % 2, 0, :], math.exp(K_CLAMP), None,
                                ALU.min).then_inc(dve_min, 1)

            def recurrence(b, c):
                t, j = divmod(c, CH)
                kv = KV[:, c % 2]
                dve.wait_ge(pe_g, CREDIT + GROUPS * b + 3 * c + 2)
                dve.wait_ge(dve_min, CHUNKS * b + c + 1)
                V.tensor_tensor(kv[:, 1, :], kv[:, 0, :], KVR[:, 1, :], ALU.mult).then_inc(dve_kv, 1)
                dve.wait_ge(dve_sum, CREDIT + CHUNKS * b + c)
                if t == 0:
                    V.memset(S[:, :, 0:1], 0.0)
                else:
                    V.tensor_copy(S[:, :, 0:1], state[:, j, :].rearrange("p (a o) -> p a o", o=1))
                dec = decay[:, j:j + 1].to_broadcast([P, TILE])
                for i in range(2):
                    if i == 1:
                        dve.wait_ge(dve_kv, CREDIT + CHUNKS * b + c + 1)
                    last = V.tensor_tensor_scan(S[:, i, 1:TILE + 1], dec, kv[:, i, :],
                                                0.0 if t == 0 else state[:, j, i:i + 1], ALU.mult, ALU.add)
                last.then_inc(dve_scan, 1)
                dve.wait_ge(dve_scan, CHUNKS * b + c + 1)
                if t == 0:
                    V.tensor_copy(state[:, j, :].rearrange("p (a o) -> p a o", o=1), S[:, :, TILE:TILE + 1])
                V.scalar_tensor_tensor(kv, kv, first[:, j:j + 1], S[:, :, 0:TILE], ALU.mult,
                                       ALU.add).then_inc(dve_sum, 1)

            def denominator(b, c):
                dve.wait_ge(act_ls, CHUNKS * b + c + 1)
                V.tensor_tensor(E[:, c % 2, :], E[:, c % 2, :], KV[:, c % 2, 0, :], ALU.add).then_inc(dve_l, 1)

            def rwkv(b, c):
                dve.wait_ge(act_y, CHUNKS * b + c + 1)
                V.tensor_tensor(KV[:, c % 2, 1, :], KV[:, c % 2, 1, :], E[:, c % 2, :], ALU.mult).then_inc(dve_rw, 1)

            def rwkv_lo(b, c):
                dve.wait_ge(act_rh, CHUNKS * b + c + 1)
                V.tensor_tensor(RL[:, c % CH, :], KV[:, c % 2, 1, :], RH[:, c % CH, :].bitcast(F32),
                                ALU.subtract).then_inc(dve_rl, 1)

            def add_out(b, ph, what, banks=None):
                use = bank_use(b, ph, what)
                t = int(what[-1])
                if what.startswith("attn") or what.startswith("own"):
                    tile = X[t]
                    for normed in (pool_xn, act_xn):
                        dve.wait_ge(normed, CREDIT + normed_count(b, f"ffn_own{t}"))
                else:
                    tile = ZB
                    dve.wait_ge(s_park, 32 * (b - HALF) + 16 * t + 16)
                if ph == "B" and what.startswith("attn"):
                    dve.wait_ge(dve_out, BANKS + bank_use(b, ph, f"own{t}") + Q)
                for q in range(Q) if banks is None else banks:
                    dve.wait_ge(pe_out, use + q + 1)
                    if what.startswith("attn"):
                        V.tensor_tensor(tile[:, q, :], tile[:, q, :], OUT[:, q, :], ALU.add).then_inc(dve_out, 1)
                    else:
                        V.scalar_tensor_tensor(tile[:, q, :], OUT[:, q, :], sc[:, 7:8], tile[:, q, :],
                                               ALU.mult, ALU.add).then_inc(dve_out, 1)

            STATS_AT = {4: "own1", 16: "next0"}
            ADDS_AT = {5: [("own0", [0])], 6: [("own0", [1])], 7: [("own0", [2, 3])],
                       9: [("other0", [0])], 10: [("other0", [1])], 11: [("other0", [2])], 12: [("other0", [3])],
                       17: [("own1", [0])], 18: [("own1", [1])], 19: [("own1", [2, 3])],
                       21: [("other1", [0, 1])], 22: [("other1", [2, 3])]}

            def batch(b, ph, is_last=False):
                last = None
                for g in range(GROUPS):
                    c, m = divmod(g, 3)
                    n = slot_ahead(g, is_last)
                    if m == 2 and c and c != CH and g != ATTN0_AFTER - 1:
                        rwkv_lo(b, c - 1)
                    part1_first = ahead_of_part2(n)
                    if part1_first:
                        mix_or_clip(b, ph, n)
                    early = ph == "B" and g == GROUPS - 1 and not is_last
                    if early:
                        denominator(b, CHUNKS - 1)
                    if last is not None:
                        low_part(b, ph, last)
                    for what, banks in (ADDS_AT.get(g, ()) if ph == "B" else ()):
                        add_out(b, ph, what, banks)
                    if g == ATTN0_AFTER:
                        recurrence(b, CH - 1)
                    if n is not None and not part1_first:
                        mix_or_clip(b, ph, n)
                    last = n
                    if g == ATTN0_AFTER - 1:
                        low_part(b, ph, last)
                        last = None
                        rwkv_lo(b, c - 1)
                    if g in STATS_AT:
                        tile_stats(b, STATS_AT[g], is_last)
                    if m == 0:
                        clamp_k(b, c)
                        if c:
                            denominator(b, c - 1)
                            if c == CH:
                                rwkv(b, c - 1)
                                rwkv_lo(b, c - 1)
                                tile_stats(b, "other1", is_last)
                                add_out(b, ph, "attn0")
                    elif m == 1:
                        if c and c != CH:
                            rwkv(b, c - 1)
                        if c != CH - 1:
                            recurrence(b, c)
                if not early:
                    denominator(b, CHUNKS - 1)
                if last is not None:
                    low_part(b, ph, last)
                rwkv(b, CHUNKS - 1)
                rwkv_lo(b, CHUNKS - 1)
                if not is_last:
                    tile_stats(b + 1, "other0", is_last)
                if ph == "A":
                    dve.wait_ge(dve_lo, RING + slots_before(b, ph, first_slot("mix_next0")))
                    V.tensor_tensor(mx[:, :], mx[:, :], am[:, :], ALU.max).then_inc(dve_mx, 1)
                add_out(b, ph, "attn1")

            with dve.Fori(0, HALF) as b:
                batch(b, "A")
            dve.wait_ge(dve_mx, HALF + 1)
            V.tensor_reduce(sc[:, 5:6], mx[:, :], AX.X, ALU.max).then_inc(dve_s, 1)
            dve.wait_ge(pool_max, 1)
            V.reciprocal(sc[:, 3:4], sc[:, 6:7]).then_inc(dve_s, 1)
            V.scalar_tensor_tensor(sc[:, 7:8], sc[:, 6:7], 1.0 / QB, sc[:, 2:3], ALU.mult, ALU.mult)
            dve.wait_ge(dve_s, 4)
            V.tensor_scalar(gamq[:, :], gam[:, :], QB, sc[:, 3:4], ALU.mult, ALU.mult)
            V.tensor_scalar(betq[:, :], bet[:, :], QB, sc[:, 3:4], ALU.mult, ALU.mult).then_inc(dve_s, 1)
            dve.wait_ge(dve_s, 5)
            with dve.Fori(HALF, B - 1) as b:
                batch(b, "B")
            batch(B - 1, "B", is_last=True)

        @block.gpsimd
        def _(pool):
            G = nc.gpsimd
            pool.sem_inc(pool_step, STEPS)
            G.memset(ident[:, :], 0.0).then_inc(pool_id, 1)
            pool.wait_ge(pool_id, 1)
            G.affine_select(out=ident[:, :], in_=ident[:, :], compare_op=ALU.not_equal, fill=1.0, base=0,
                            pattern=[[-1, P]], channel_multiplier=1).then_inc(pool_id, 1)

            def step(i, k, instruction):
                instruction.then_inc(pool_step, 1)
                pool.wait_ge(pool_step, STEPS + i * STEPS + k)
                pool.sem_inc(pool_past, 1)

            def mix_scale(i, r, dst):
                mean, var = mv[:, r, :, 0], mv[:, r, :, 1]
                pool.wait_ge(dve_mv, i + 1)
                pool.sem_inc(pool_past, 1)
                G.tensor_scalar(st[:, 5, :], mean, -1.0, 0.0, ALU.mult, ALU.add)
                step(i, 1, G.tensor_scalar(st[:, 0, :], var, 1.0, LN_EPS, ALU.mult, ALU.add))
                step(i, 2, G.tensor_tensor(dst[:, 0, :], st[:, 0, :], half_neg[:, :], ALU.pow))
                step(i, 3, G.tensor_tensor(dst[:, 1, :], st[:, 5, :], dst[:, 0, :], ALU.mult))

            def ffn_scale(i, r, dst):
                var = mv[:, r, :, 1]
                step(i, 4, G.tensor_tensor(st[:, 1, :], var, dst[:, 0, :], ALU.mult))
                step(i, 5, G.tensor_tensor(st[:, 2, :], st[:, 1, :], dst[:, 0, :], ALU.mult))
                step(i, 6, G.tensor_scalar(st[:, 3, :], st[:, 2, :], 1.0, FFN_LN_EPS, ALU.mult, ALU.add))
                step(i, 7, G.tensor_tensor(st[:, 4, :], st[:, 3, :], half_neg[:, :], ALU.pow))
                step(i, 8, G.tensor_tensor(dst[:, 2, :], st[:, 4, :], dst[:, 0, :], ALU.mult))
                step(i, STEPS, G.tensor_tensor(dst[:, 3, :], st[:, 5, :], dst[:, 2, :], ALU.mult))

            def normalise(dst, src, stats, ffn, done, chunks=POOL_CHUNKS):
                pool.sem_inc(pool_past, 1)
                for q in chunks:
                    last = G.tensor_scalar(dst[:, q, :], src[:, q, :], stats[:, 2 * ffn, q:q + 1],
                                           stats[:, 2 * ffn + 1, q:q + 1], ALU.mult, ALU.add)
                last.then_inc(done, 1)

            pool.wait_ge(dve_c, 1)
            mix_scale(0, 0, own[:, 0])
            normalise(XN, X[0], own[:, 0], 0, pool_xn, range(Q))
            ffn_scale(0, 0, own[:, 0])
            pool.wait_ge(pe_t, CH)
            normalise(XN, X[0], own[:, 0], 1, pool_xn, range(Q))
            pool.wait_ge(dve_q, 1)
            G.partition_all_reduce(sc[:, 1:2], sc[:, 0:1], P, bass.bass_isa.ReduceOp.add).then_inc(pool_sum, 1)

            def call(b, tile):
                return stats_number(b, tile), (STATS_ORDER.index(tile) + 1) % 2

            def other(b, tile):
                mix_scale(*call(b, tile), oth)
                ffn_scale(*call(b, tile), oth)
                normalise(ZA, ZA, oth, 1, pool_za)

            def batch(b, is_last=False, other_ahead=True):
                mix_scale(*call(b, "own1"), own[:, 1])
                pool.wait_ge(pe_t, slots_before(b, "any", first_slot("ffn_own0") + CH))
                normalise(XN, X[1], own[:, 1], 0, pool_xn)
                ffn_scale(*call(b, "own1"), own[:, 1])
                pool.wait_ge(pe_t, slots_before(b, "any", first_slot("mix_own1") + CH))
                normalise(XN, X[1], own[:, 1], 1, pool_xn)
                other(b, "other1")
                if not is_last:
                    mix_scale(*call(b, "next0"), own[:, 0])
                    pool.wait_ge(pe_t, slots_before(b, "any", first_slot("ffn_own1") + CH))
                    normalise(XN, X[0], own[:, 0], 0, pool_xn)
                    ffn_scale(*call(b, "next0"), own[:, 0])
                    pool.wait_ge(pe_t, slots_before(b, "any", len(SLOTS)))
                    normalise(XN, X[0], own[:, 0], 1, pool_xn)
                    if other_ahead:
                        other(b + 1, "other0")

            other(0, "other0")
            with pool.Fori(0, HALF - 1) as b:
                batch(b)
            batch(HALF - 1, other_ahead=False)
            pool.wait_ge(dve_s, 3)
            G.partition_all_reduce(sc[:, 6:7], sc[:, 5:6], P, bass.bass_isa.ReduceOp.max).then_inc(pool_max, 1)
            other(HALF, "other0")
            with pool.Fori(HALF, B - 1) as b:
                batch(b)
            batch(B - 1, is_last=True)


_INS = ["L0_attn_x", "L0_attn_time_decay", "L0_attn_time_first", "L0_attn_time_mix", "L0_attn_Wk",
        "L0_attn_Wv", "L0_attn_Wr", "L0_attn_Wo", "L0_ffn_weight", "L0_ffn_ln_gamma", "L0_ffn_ln_beta"]


def kernel(**inputs):
    import numpy as np
    import concourse.bacc as bacc
    from concourse.bass_utils import run_bass_kernel_spmd

    nc = bacc.Bacc("TRN2", target_bir_lowering=False, num_devices=1)
    arrays, args = {}, []
    for name in _INS:
        a = np.ascontiguousarray(inputs[name])
        arrays[f"in_{name}"] = a
        args.append(nc.dram_tensor(f"in_{name}", a.shape, mybir.dt.from_np(a.dtype), kind="ExternalInput").ap())
    shape = arrays["in_L0_attn_x"].shape
    result = nc.dram_tensor("out", shape, F32, kind="ExternalOutput").ap()
    mixed_decay_kernel(nc, *args, result)
    r = run_bass_kernel_spmd(nc, [arrays], core_ids=[0])
    return r.results[0]["out"]
```
